# Optimizing a Trainium2 kernel written in Bass

```python
import numpy as np
import jax
import jax.numpy as jnp

def _softmax(x, axis=-1):
    return jax.nn.softmax(x, axis=axis)

def _gelu(x):
    return jax.nn.gelu(x, approximate=True)

def _silu(x):
    return jax.nn.silu(x)

def _sigmoid(x):
    return jax.nn.sigmoid(x)

def _layernorm(x, axis=-1, eps=1e-05):
    m = jnp.mean(x, axis=axis, keepdims=True)
    v = jnp.var(x, axis=axis, keepdims=True)
    return (x - m) / jnp.sqrt(v + eps)

def _scatter_add(tgt, idx, src, axis=0):
    return tgt.at[idx].add(src)

def _segment_sum(src, seg, n):
    return jax.ops.segment_sum(src, seg, n)
kernel_name = 'mk_adaln_ffn_d1_seqx_r4_5d9366'

def setup_inputs(seed: int=0):
    np.random.seed(seed)
    _w = jnp.asarray

    def _rec_inputs():
        import jax
        import jax.numpy as jnp
        _rk = jax.random.key(seed)
        x = -0.0003929 + 0.9999 * jax.random.normal(jax.random.fold_in(_rk, 1), (8, 256, 256), jnp.float32)
        _lenS = 256 - jax.random.randint(jax.random.fold_in(_rk, 7), (8,), 0, max(1, 256 // 4) + 1, jnp.int32)
        _lenS2 = 256 - jax.random.randint(jax.random.fold_in(_rk, 8), (8,), 0, max(1, 256 // 4) + 1, jnp.int32)
        cond_256 = -0.0209273 + 1.04763 * jax.random.normal(jax.random.fold_in(_rk, 11), (8, 64), jnp.float32)
        return (x, cond_256)
    x, cond_256 = _rec_inputs()

    def _L0_cond_setup():
        import jax, jax.numpy as jnp
        import numpy as np
        EPS = 1e-08

        def hamilton(q1, q2):
            w1, x1, y1, z1 = (q1[..., i, :] for i in range(4))
            w2, x2, y2, z2 = (q2[..., i, :] for i in range(4))
            w = w1 * w2 - x1 * x2 - y1 * y2 - z1 * z2
            x = w1 * x2 + x1 * w2 + y1 * z2 - z1 * y2
            y = w1 * y2 - x1 * z2 + y1 * w2 + z1 * x2
            z = w1 * z2 + x1 * y2 - y1 * x2 + z1 * w2
            return jnp.stack([w, x, y, z], axis=-2)

        def _normalize(q):
            return q / jnp.sqrt(jnp.sum(q * q, axis=0, keepdims=True) + EPS)
        key = jax.random.key(seed)
        k1, k2, k3, k4 = jax.random.split(key, 4)
        B, T, d_model = (4, 1024, 256)
        quat_dim = d_model // 4
        x = jax.random.normal(k1, (B, T, d_model), dtype=jnp.float32)
        q_left = jax.random.normal(k2, (4, quat_dim), dtype=jnp.float32)
        q_right = jax.random.normal(k3, (4, quat_dim), dtype=jnp.float32)
        spectral_gate = jax.random.uniform(k4, (1, 1, 1, quat_dim), dtype=jnp.float32)
        return {'x': x, 'q_left': q_left, 'q_right': q_right, 'spectral_gate': spectral_gate}
    _L0_cond_all = _L0_cond_setup()
    _L0_cond_in = {k: v for k, v in _L0_cond_all.items() if k in ('q_right', 'spectral_gate')}
    del _L0_cond_all

    def _L0_ffn_setup():
        import jax, jax.numpy as jnp
        import numpy as np
        DIM = 256
        HIDDEN = 1024
        E = 8
        B, S = (2, 1024)
        key = jax.random.key(seed)
        ks = jax.random.split(key, 8)
        sd = 1.0 / np.sqrt(DIM)
        sh = 1.0 / np.sqrt(HIDDEN)
        return {'x': jax.random.normal(ks[0], (B, S, DIM), dtype=jnp.float32), 'router_w': jax.random.uniform(ks[1], (DIM, E), jnp.float32, -sd, sd), 'router_b': jax.random.uniform(ks[2], (E,), jnp.float32, -sd, sd), 'w1': jax.random.uniform(ks[3], (E, DIM, 2 * HIDDEN), jnp.float32, -sd, sd), 'b1': jax.random.uniform(ks[4], (E, 2 * HIDDEN), jnp.float32, -sd, sd), 'w2': jax.random.uniform(ks[5], (E, HIDDEN, DIM), jnp.float32, -sh, sh), 'b2': jax.random.uniform(ks[6], (E, DIM), jnp.float32, -sh, sh)}
    _L0_ffn_all = _L0_ffn_setup()
    _L0_ffn_in = {k: v for k, v in _L0_ffn_all.items() if k in ('router_w', 'router_b', 'w1', 'b1', 'w2', 'b2')}
    del _L0_ffn_all
    return {'x': x, 'cond_256': cond_256, 'L0_cond_q_right': _L0_cond_in['q_right'], 'L0_cond_spectral_gate': _L0_cond_in['spectral_gate'], 'L0_ffn_router_w': _L0_ffn_in['router_w'], 'L0_ffn_router_b': _L0_ffn_in['router_b'], 'L0_ffn_w1': _L0_ffn_in['w1'], 'L0_ffn_b1': _L0_ffn_in['b1'], 'L0_ffn_w2': _L0_ffn_in['w2'], 'L0_ffn_b2': _L0_ffn_in['b2']}

def reference(x, cond_256, L0_cond_q_right, L0_cond_spectral_gate, L0_ffn_router_w, L0_ffn_router_b, L0_ffn_w1, L0_ffn_b1, L0_ffn_w2, L0_ffn_b2):
    import jax
    import jax.numpy as jnp

    def _L0_cond_ref(x, q_left, q_right, spectral_gate):
        import jax, jax.numpy as jnp
        import numpy as np
        EPS = 1e-08

        def hamilton(q1, q2):
            w1, x1, y1, z1 = (q1[..., i, :] for i in range(4))
            w2, x2, y2, z2 = (q2[..., i, :] for i in range(4))
            w = w1 * w2 - x1 * x2 - y1 * y2 - z1 * z2
            x = w1 * x2 + x1 * w2 + y1 * z2 - z1 * y2
            y = w1 * y2 - x1 * z2 + y1 * w2 + z1 * x2
            z = w1 * z2 + x1 * y2 - y1 * x2 + z1 * w2
            return jnp.stack([w, x, y, z], axis=-2)

        def _normalize(q):
            return q / jnp.sqrt(jnp.sum(q * q, axis=0, keepdims=True) + EPS)
        B, T, d_model = x.shape
        quat_dim = d_model // 4
        x_quat = x.reshape(B, T, 4, quat_dim)
        x_spectral = jnp.fft.fft(x_quat, axis=1)
        x_filtered = jnp.fft.ifft(x_spectral * spectral_gate, axis=1).real.astype(x.dtype)
        q_left_n = _normalize(q_left)
        q_right_n = _normalize(q_right)
        conj_sign = jnp.array([1.0, -1.0, -1.0, -1.0], dtype=x.dtype)[:, None]
        q_right_conj = q_right_n * conj_sign
        x_right = hamilton(x_filtered, q_right_conj)
        x_rotated = hamilton(q_left_n, x_right)
        return x_rotated.reshape(B, T, d_model)

    def _L0_ffn_ref(x, router_w, router_b, w1, b1, w2, b2):
        import jax, jax.numpy as jnp
        import numpy as np
        DIM = 256
        HIDDEN = 1024
        E = 8
        B, S = (2, 1024)
        logits = jnp.einsum('bsd,de->bse', x, router_w) + router_b
        probs = jax.nn.softmax(logits, axis=-1)
        top1 = jnp.argmax(probs, axis=-1)
        out = jnp.zeros_like(x)
        for i in range(E):
            h = jnp.einsum('bsd,df->bsf', x, w1[i]) + b1[i]
            a, g = jnp.split(h, 2, axis=-1)
            y = jnp.einsum('bsh,hd->bsd', a * jax.nn.sigmoid(g), w2[i]) + b2[i]
            out = out + jnp.where((top1 == i)[..., None], y, 0.0)
        return out
    x = x + _L0_ffn_ref(_L0_cond_ref(x, cond_256, L0_cond_q_right, L0_cond_spectral_gate), L0_ffn_router_w, L0_ffn_router_b, L0_ffn_w1, L0_ffn_b1, L0_ffn_w2, L0_ffn_b2)
    return x

_drawn_inputs = setup_inputs


def setup_inputs(seed=0):
    import zlib

    import numpy as np

    out = dict(_drawn_inputs(seed))
    spreads = {}
    factors = {'L0_ffn_b1': 5.418, 'L0_ffn_b2': 3.088}
    for name, (base, spread) in spreads.items():
        noise = np.random.default_rng([zlib.crc32(name.encode()), seed]).standard_normal(out[name].shape)
        drawn = base * np.exp(spread * noise) if base else spread * noise
        out[name] = jnp.asarray(drawn.astype(out[name].dtype))
    for name, factor in factors.items():
        out[name] = (out[name] * factor).astype(out[name].dtype)
    return out
```

```python
import concourse.bass as bass
from concourse import mybir
from contextlib import ExitStack


def adaln_moe_ffn_kernel(nc, x, cond, q_right, gate, router_w, router_b, w1, b1, w2, b2, out):
    F32 = mybir.dt.float32
    F32R = mybir.dt.float32r
    BF16 = mybir.dt.bfloat16
    I32 = mybir.dt.int32
    U32 = mybir.dt.uint32
    ALU = mybir.AluOpType
    ACT = mybir.ActivationFunctionType
    AX = mybir.AxisListType

    P = 128
    BATCH, SEQ, DIM = x.shape
    TOK = BATCH * SEQ
    NB = TOK // P
    NE = router_w.shape[1]
    HID = w2.shape[1]
    QC = 4
    QD = DIM // QC
    KH = DIM // P
    JH = QD // KH
    NC = HID // P
    ITEM = 256
    NSUB = ITEM // P
    STEP = 64
    NSTEP = ITEM // STEP
    MAX_ITEMS = TOK // ITEM + NE - 1
    TAB = MAX_ITEMS + 3
    UNIT = 1024
    W1U = KH * 2 * HID // UNIT
    W2U = HID // P * DIM // UNIT
    WU = W1U + W2U
    CPU2 = UNIT // DIM
    RING = 4
    BIG = 4096
    EPS = 1e-8

    x_flat = x.rearrange("b s d -> (b s) d")
    out_flat = out.rearrange("b s d -> (b s) d")

    ctx = ExitStack()
    with ctx:
        def sb(name, cols, dt=F32, rows=P):
            return ctx.enter_context(nc.sbuf_tensor(name, [rows, cols], dt))

        def ps(name):
            return ctx.enter_context(nc.psum_tensor(name, [P, 512], F32))

        def sem(name):
            return ctx.enter_context(nc.semaphore(name))

        w_raw = sb("w_raw", WU * UNIT)
        w_hi = sb("w_hi", 2 * WU * UNIT, F32R)
        w_lo = sb("w_lo", 2 * WU * UNIT, F32R)
        arena = sb("arena", NB * DIM)
        x_tok = arena[:, :].rearrange("p (n d) -> p n d", n=NB)
        u32 = arena[:, 0:NC * ITEM].rearrange("p (c t) -> p c t", c=NC)
        sig = arena[:, NC * ITEM:NC * ITEM + RING * ITEM].rearrange("p (c t) -> p c t", c=RING)
        arena_t = sb("arena_t", NB * DIM)
        x_t = arena_t[:, :].rearrange("p (n k t) -> p n k t", n=NB, k=KH)
        xb = arena_t[:, 0:4 * NSUB * DIM]
        u_hi = sb("u_hi", NC * ITEM, F32R)
        u_lo = sb("u_lo", NC * ITEM, F32R)
        xr_hi = sb("xr_hi", 2 * KH * ITEM, F32R)
        xr_lo = sb("xr_lo", 2 * KH * ITEM, F32R)
        xg = sb("xg", NSUB * DIM)
        xg_t = sb("xg_t", KH * ITEM)
        y_out = sb("y_out", NSUB * DIM)
        b1_rows = sb("b1_rows", P)
        b1_t = sb("b1_t", P)
        b1_cur = sb("b1_cur", 2 * NC)
        b2_all = sb("b2_all", NE * DIM)
        g_cur = sb("g_cur", NSUB, I32)
        s_cur = sb("s_cur", NSUB, I32)
        g_idx = sb("g_idx", TAB * NSUB, I32)
        s_idx = sb("s_idx", TAB * NSUB, I32)
        ctrl = sb("ctrl", 2 + TAB, I32)
        ident = sb("ident", P)
        iota = sb("iota", P)
        lower = sb("lower", P, BF16)
        ones16 = sb("ones16", P, BF16)
        ones = sb("ones", P)
        pcol = sb("pcol", 1)
        rev = sb("rev", NE)
        m4i = sb("m4i", TAB)
        sgn_l = sb("sgn_l", 64)
        sgn_r = sb("sgn_r", 64)
        mask_j = sb("mask_j", JH)
        mask_c = sb("mask_c", QC)
        q_rows = sb("q_rows", QD, rows=13)
        q_rep = sb("q_rep", KH * P, rows=13)
        qv = sb("qv", KH * 16)
        qsq = sb("qsq", KH * 16)
        nrm = sb("nrm", 4 * KH * 2)
        mats = sb("mats", 2 * KH * 16)
        prod = sb("prod", KH * 64)
        r_full = sb("r_full", KH * 16)
        coef = sb("coef", KH * QC)
        rot = sb("rot", KH * P)
        rot_t = sb("rot_t", KH * P)
        wr = sb("wr", KH * NE)
        wr_rot = sb("wr_rot", KH * NE)
        rb = sb("rb", NE)
        lg = sb("lg", NB * NE)
        eq = sb("eq", NB * NE)
        mx = sb("mx", NB)
        oh = sb("oh", NB * NE, BF16)
        gin = sb("gin", NB * NE)
        gex = sb("gex", NB * NE)
        pos = sb("pos", NB * NE)
        sm = sb("sm", 8 * NE)
        slot = sb("slot", NB, I32)
        slot_q = sb("slot_q", NB, I32)
        slot_r = sb("slot_r", NB, I32)
        idx_f = sb("idx_f", 3 * TAB * NSUB)

        def part(a, at, cols):
            return a[:, at:at + cols]

        ct = part(arena, NC * ITEM + RING * ITEM, 4 * TAB * NE)
        cv = part(arena, NC * ITEM + RING * ITEM + 4 * TAB * NE, 8 * TAB)
        q_oh = part(arena, NC * ITEM + RING * ITEM + 4 * TAB * NE + 8 * TAB, NB * TAB * NSUB // 2).bitcast(BF16)
        slot_oh = part(arena_t, 4 * NSUB * DIM, NB * P // 2).bitcast(BF16).rearrange("p (n r) -> p n r", n=NB)
        q_val = part(arena_t, 4 * NSUB * DIM + NB * P // 2, NB * TAB * NSUB).bitcast(BF16)

        pair = [ps(f"pair{b}") for b in range(RING)]
        y_ps = ps("y_ps")
        xt_ps = ps("xt_ps")
        xr_ps = ps("xr_ps")
        rt_ps = ps("rt_ps")

        consts_ready = sem("consts_ready")
        pool_chain = sem("pool_chain")
        dve_chain = sem("dve_chain")
        q_loaded = sem("q_loaded")
        small_loaded = sem("small_loaded")
        b2_loaded = sem("b2_loaded")
        x_loaded = [sem(f"x_loaded{g}") for g in range(4)]
        w_loaded = [sem(f"w_loaded{u}") for u in range(WU)]
        q_repeated = sem("q_repeated")
        q_spread = sem("q_spread")
        sums_ready = sem("sums_ready")
        roots_ready = sem("roots_ready")
        rot_ready = sem("rot_ready")
        rot_turned = sem("rot_turned")
        rot_t_ready = sem("rot_t_ready")
        wr_turned = sem("wr_turned")
        wr_ready = sem("wr_ready")
        b1_turned = sem("b1_turned")
        x_turned = sem("x_turned")
        x_t_even = sem("x_t_even")
        x_t_odd = sem("x_t_odd")
        logits_ready = sem("logits_ready")
        oh_ready = sem("oh_ready")
        ranks_ready = sem("ranks_ready")
        slots_ready = sem("slots_ready")
        idx_summed = sem("idx_summed")
        ctrl_ready = sem("ctrl_ready")
        idx_ready = sem("idx_ready")
        w1_hi_done = sem("w1_hi_done")
        w2_hi_done = sem("w2_hi_done")
        w1_split = sem("w1_split")
        w2_split = sem("w2_split")
        gathered = sem("gathered")
        scattered = sem("scattered")
        xb_done = sem("xb_done")
        xg_turned = sem("xg_turned")
        xg_t_done = sem("xg_t_done")
        rotated = sem("rotated")
        xr_hi_done = sem("xr_hi_done")
        xr_lo_done = sem("xr_lo_done")
        b1_cur_done = sem("b1_cur_done")
        mm1_done = sem("mm1_done")
        sig_done = sem("sig_done")
        pair_free = sem("pair_free")
        u_hi_done = sem("u_hi_done")
        u_lo_done = sem("u_lo_done")
        mm2_done = sem("mm2_done")
        y_done = sem("y_done")

        block = ctx.enter_context(nc.Block())

        def w_col(parity, unit):
            return parity * (WU * UNIT) + unit * UNIT

        def f_steps(w):
            return w & 3

        def f_two(w):
            return (w >> 1) & 1

        def f_prep(w):
            return (w >> 2) & 1

        def f_first(w):
            return (w >> 3) & 1

        def f_expert(w):
            return (w >> 4).with_bounds(min_val=0, max_val=NE - 1)

        def load_last(eng):
            return eng.value_load(ctrl[0:1, 0:1], min_val=NE - 1, max_val=MAX_ITEMS - 1)

        def load_word(eng, i):
            return eng.value_load(ctrl[0:1, bass.ds(i + 2, 1)], min_val=0, max_val=127)

        @block.sync
        def _(sp):
            sp.dma_start(q_rows[0:8, :], cond).then_inc(q_loaded, 16)
            sp.dma_start(q_rows[8:12, :], q_right).then_inc(q_loaded, 16)
            sp.dma_start(q_rows[12:13, :], gate.rearrange("a b c j -> (a b c) j")).then_inc(q_loaded, 16)
            xv = x_flat.rearrange("(p n) d -> p n d", p=P)
            for g in range(4):
                sp.dma_start(x_tok[:, 4 * g:4 * g + 4, :], xv[:, 4 * g:4 * g + 4, :]).then_inc(x_loaded[g], 16)

            w1_v = w1.rearrange("e (m k) (ag f) -> e m (k ag) f", k=KH, ag=2)
            w2_v = w2.rearrange("e (h c p) d -> e h p c d", h=W2U, p=P)

            def load_unit(e, u):
                if u < W1U:
                    dst = w_raw[:, u * UNIT:(u + 1) * UNIT].rearrange("p (b f) -> p b f", b=2 * KH)
                    sp.dma_start(dst, w1_v[e, :, :, u * 256:(u + 1) * 256]).then_inc(w_loaded[u], 16)
                else:
                    dst = w_raw[:, u * UNIT:(u + 1) * UNIT].rearrange("p (c d) -> p c d", d=DIM)
                    sp.dma_start(dst, w2_v[e, u - W1U]).then_inc(w_loaded[u], 16)

            for u in range(WU):
                load_unit(0, u)
            with sp.Fori(1, NE) as e:
                for u in range(WU):
                    if u < W1U:
                        sp.wait_ge(w1_split, e * W1U - (W1U - u - 1))
                    else:
                        sp.wait_ge(w2_split, e * W2U - (W2U - (u - W1U) - 1))
                    load_unit(e, u)

        @block.gpsimd
        def _(pool):
            count = [0]

            def link(ins):
                count[0] += 1
                ins.then_inc(pool_chain, 1)
                pool.wait_ge(pool_chain, count[0])

            nc.gpsimd.memset(ones[:, :], 1.0).then_inc(pool_chain, 1)
            nc.gpsimd.memset(ones16[:, :], 1.0).then_inc(pool_chain, 1)
            nc.gpsimd.memset(sgn_l[:, :], 0.0).then_inc(pool_chain, 1)
            nc.gpsimd.memset(sgn_r[:, :], 0.0).then_inc(pool_chain, 1)
            nc.gpsimd.memset(y_out[:, :], 0.0).then_inc(pool_chain, 1)
            count[0] = 5
            pool.wait_ge(pool_chain, count[0])
            nc.gpsimd.affine_select(out=ident[:, :], in_=ones[:, :], compare_op=ALU.is_equal, fill=0.0,
                                    base=0, pattern=[[-1, P]], channel_multiplier=1).then_inc(consts_ready, 1)
            left = ((1, -1, -1, -1), (1, 1, -1, 1), (1, 1, 1, -1), (1, -1, 1, 1))
            right = ((1, -1, -1, -1), (1, 1, 1, -1), (1, -1, 1, 1), (1, 1, -1, 1))
            for a in range(QC):
                for b in range(QC):
                    m = a ^ b
                    conj = 1 if m == 0 else -1
                    nc.gpsimd.memset(sgn_l[:, a * 16 + b * 4 + m:a * 16 + b * 4 + m + 1], float(left[a][b]))
                    last = nc.gpsimd.memset(sgn_r[:, a * 16 + b * 4 + m:a * 16 + b * 4 + m + 1],
                                            float(right[a][b] * conj))
            last.then_inc(consts_ready, 1)
            nc.gpsimd.iota(iota[:, :], pattern=[[1, P]], base=0, channel_multiplier=0,
                           allow_small_or_imprecise_dtypes=True).then_inc(consts_ready, 1)
            nc.gpsimd.iota(pcol[:, :], pattern=[[0, 1]], base=1, channel_multiplier=1,
                           allow_small_or_imprecise_dtypes=True).then_inc(consts_ready, 1)
            nc.gpsimd.affine_select(out=lower[:, :], in_=ones16[:, :], compare_op=ALU.is_ge, fill=0.0,
                                    base=-1, pattern=[[1, P]], channel_multiplier=-1).then_inc(consts_ready, 1)

            def lo_unit(parity, u, done, hi_done, n_hi):
                pool.wait_ge(hi_done, n_hi)
                nc.gpsimd.tensor_tensor(w_lo[:, bass.ds(w_col(parity, u), UNIT)],
                                        w_raw[:, u * UNIT:(u + 1) * UNIT],
                                        w_hi[:, bass.ds(w_col(parity, u), UNIT)].bitcast(F32),
                                        ALU.subtract).then_inc(done, 1)

            for u in range(W1U):
                lo_unit(0, u, w1_split, w1_hi_done, u + 1)

            pool.wait_ge(idx_ready, 1)
            pool.wait_ge(ctrl_ready, 1)
            last_item = load_last(pool)

            row_bound = pool.to_reg(TOK - 1)

            def issue_gather(idx):
                for s in range(NSUB):
                    nc.gpsimd.indirect_dma_start(
                        out=xg[:, s * DIM:(s + 1) * DIM], out_offset=None, in_=x_flat,
                        in_offset=bass.IndirectOffsetOnAxis(ap=idx[:, s:s + 1], axis=0),
                        bounds_check=row_bound, oob_is_err=False).then_inc(gathered, 16)

            def add_b2(i, word):
                e = f_expert(word)
                dst = xb[:, bass.ds((i & 3) * (NSUB * DIM), NSUB * DIM)]
                nc.gpsimd.tensor_tensor(
                    dst.rearrange("p (s d) -> p s d", s=NSUB),
                    xg[:, :].rearrange("p (s d) -> p s d", s=NSUB),
                    b2_all[:, bass.ds(e * DIM, DIM)].unsqueeze(1).to_broadcast([P, NSUB, DIM]),
                    ALU.add).then_inc(xb_done, 1)

            issue_gather(g_idx[:, 0:NSUB])
            pool.wait_ge(b2_loaded, 16)
            pool.wait_ge(gathered, 16 * NSUB)
            add_b2(0, load_word(pool, 0))
            pool.wait_ge(xb_done, 1)
            pool.wait_ge(xg_turned, 1)
            issue_gather(g_idx[:, NSUB:2 * NSUB])
            for u in range(W2U):
                lo_unit(0, W1U + u, w2_split, w2_hi_done, u + 1)

            base = count[0]

            def scatter(i, step):
                pool.wait_ge(y_done, i + 1)
                nc.gpsimd.tensor_copy(s_cur[:, :], s_idx[:, bass.ds(i * NSUB, NSUB)]).then_inc(pool_chain, 1)
                step = pool.to_reg(step)
                pool.wait_ge(idx_ready, 1)
                pool.wait_ge(pool_chain, step)
                for s in range(NSUB):
                    nc.gpsimd.indirect_dma_start(
                        out=out_flat, out_offset=bass.IndirectOffsetOnAxis(ap=s_cur[:, s:s + 1], axis=0),
                        in_=y_out[:, s * DIM:(s + 1) * DIM], in_offset=None,
                        bounds_check=row_bound, oob_is_err=False).then_inc(scattered, 16)

            def item(i):
                word = load_word(pool, i)
                if not isinstance(i, int):
                    pool.wait_ge(scattered, i * (16 * NSUB) - 16 * NSUB)
                pool.wait_ge(gathered, i * (16 * NSUB) + 32 * NSUB)
                add_b2(i + 1, load_word(pool, i + 1))
                pool.wait_ge(xb_done, i + 2)
                pool.wait_ge(xg_turned, i + 2)
                nc.gpsimd.tensor_copy(g_cur[:, :], g_idx[:, bass.ds(i * NSUB + 2 * NSUB, NSUB)])\
                    .then_inc(pool_chain, 1)
                step = base + 1 if isinstance(i, int) and i == 0 else pool.to_reg(i * 2 + base)
                pool.wait_ge(idx_ready, 1)
                pool.wait_ge(pool_chain, step)
                issue_gather(g_cur)
                if not (isinstance(i, int) and i == 0):
                    scatter(i - 1, i * 2 + (base + 1))
                with pool.If(f_prep(word) > 0):
                    e = f_expert(word)
                    for u in range(W2U):
                        lo_unit((e + 1) & 1, W1U + u, w2_split, w2_hi_done, e * W2U + W2U + u + 1)

            item(0)
            item(1)
            with pool.Fori(2, MAX_ITEMS) as i:
                with pool.If(i <= last_item):
                    item(i)
            scatter(last_item, last_item * 2 + (base + 2))
            pool.wait_ge(scattered, last_item * (16 * NSUB) + 16 * NSUB)
            pool.wait_ge(gathered, last_item * (16 * NSUB) + 48 * NSUB)

        @block.scalar
        def _(act):
            act.dma_start(wr[:, :], router_w.rearrange("(m k) e -> m (k e)", k=KH)).then_inc(small_loaded, 16)
            act.dma_start(rb[:, :], router_b.partition_broadcast(P)).then_inc(small_loaded, 16)
            act.dma_start(b1_rows[:, :], b1.rearrange("e (c f) -> (e c) f", f=P)).then_inc(small_loaded, 16)
            act.dma_start(b2_all[:, :], b2.rearrange("e d -> (e d)").partition_broadcast(P)).then_inc(b2_loaded, 16)

            act.wait_ge(sums_ready, 1)
            nc.scalar.activation(nrm[:, 4:8], nrm[:, 0:4], ACT.Sqrt).then_inc(roots_ready, 1)

            for f in range(1, NB // 2, 2):
                act.wait_ge(x_turned, f + 1)
                nc.scalar.activation(arena_t[:, f * 512:(f + 1) * 512], pair[f % RING][:, :], ACT.Copy)\
                    .then_inc(x_t_odd, 1)

            def hi_unit(parity, u, n_loaded):
                act.wait_ge(w_loaded[u], n_loaded)
                nc.scalar.activation(w_hi[:, bass.ds(w_col(parity, u), UNIT)], w_raw[:, u * UNIT:(u + 1) * UNIT],
                                     ACT.Copy).then_inc(w1_hi_done if u < W1U else w2_hi_done, 1)

            for u in range(WU):
                hi_unit(0, u, 16)

            def split_x(i):
                act.wait_ge(rotated, i + 1)
                nc.scalar.activation(xr_hi[:, bass.ds((i & 1) * (KH * ITEM), KH * ITEM)], xr_ps[:, :], ACT.Copy)\
                    .then_inc(xr_hi_done, 1)

            split_x(0)
            act.wait_ge(ctrl_ready, 1)
            last_item = load_last(act)

            def gates(i, c, n):
                act.wait_ge(mm1_done, i * NC + (c + 1))
                nc.scalar.activation(sig[:, c % RING, 0:n], pair[c % RING][:, ITEM:ITEM + n], ACT.Sigmoid,
                                     bias=b1_cur[:, NC + c:NC + c + 1]).then_inc(sig_done, 1)

            def hi_u(i, g, n):
                act.wait_ge(pair_free, i * NC + (RING + 2 * g + 2))
                nc.scalar.activation(u_hi[:, 2 * g * ITEM:(2 * g + 2) * ITEM].rearrange("p (c t) -> p c t", c=2)[:, :, 0:n],
                                     u32[:, 2 * g:2 * g + 2, 0:n], ACT.Copy).then_inc(u_hi_done, 1)

            def item(i, word, n, prep, first=False):
                e = 0 if first else f_expert(word)
                act.wait_ge(b1_cur_done, e + 1)
                for c in range(RING):
                    gates(i, c, n)
                    if prep and c < W1U:
                        hi_unit((e + 1) & 1, c, e * 16 + 32)
                split_x(i + 1)
                if not first:
                    act.wait_ge(mm2_done, i)
                hi_u(i, 0, n)
                hi_u(i, 1, n)
                for c in range(RING, NC):
                    gates(i, c, n)
                    if prep and c - RING < W2U:
                        hi_unit((e + 1) & 1, W1U + c - RING, e * 16 + 32)
                    if c % 2 == 1 and c > RING + 1:
                        hi_u(i, c // 2 - 1, n)
                hi_u(i, NC // 2 - 1, n)

            word = load_word(act, 0)
            with act.If(f_two(word) > 0):
                item(0, word, ITEM, True, first=True)
            with act.Else():
                item(0, word, P, True, first=True)
            with act.Fori(1, MAX_ITEMS) as i:
                with act.If(i <= last_item):
                    word = load_word(act, i)
                    with act.If(f_prep(word) > 0):
                        with act.If(f_two(word) > 0):
                            item(i, word, ITEM, True)
                        with act.Else():
                            item(i, word, P, True)
                    with act.Else():
                        with act.If(f_two(word) > 0):
                            item(i, word, ITEM, False)
                        with act.Else():
                            item(i, word, P, False)

        @block.vector
        def _(dve):
            count = [0]

            def link(ins):
                count[0] += 1
                ins.then_inc(dve_chain, 1)
                dve.wait_ge(dve_chain, count[0])

            V = nc.vector
            dve.wait_ge(q_loaded, 48)
            for k in range(KH):
                V.tensor_copy(q_rep[:, k * P:(k + 1) * P].rearrange("r (c j) -> r c j", c=QC),
                              q_rows[:, :].rearrange("r (j k) -> r k j", k=KH)[:, k].unsqueeze(1)
                              .to_broadcast([13, QC, JH])).then_inc(q_repeated, 1)
            dve.wait_ge(consts_ready, 5)
            V.tensor_reduce(mask_j[:, :], ident[:, :].rearrange("p (c j) -> p j c", c=QC), AX.X, ALU.add)
            V.tensor_reduce(mask_c[:, :], ident[:, :].rearrange("p (c j) -> p c j", c=QC), AX.X, ALU.add)
            V.tensor_scalar(rev[:, :], iota[:, 0:NE], -1.0, float(NE), ALU.mult, ALU.add)
            V.tensor_scalar(m4i[:, :], iota[:, 0:TAB], -float(NSTEP), None, ALU.mult)
            dve.wait_ge(q_spread, 1)
            link(V.tensor_copy(qv[:, :], rt_ps[:, 0:KH * 16]))
            q3 = qv[:, :].rearrange("p (k r) -> p k r", k=KH)
            s3 = qsq[:, :].rearrange("p (k r) -> p k r", k=KH)
            link(V.tensor_tensor(qsq[:, :], qv[:, :], qv[:, :], ALU.mult))
            n3 = nrm[:, 0:4].rearrange("p (k s) -> p k s", k=KH)
            V.tensor_reduce(n3[:, :, 0], s3[:, :, 0:8], AX.X, ALU.add)
            link(V.tensor_reduce(n3[:, :, 1], s3[:, :, 8:12], AX.X, ALU.add))
            V.tensor_scalar(nrm[:, 0:4], nrm[:, 0:4], EPS, None, ALU.add).then_inc(sums_ready, 1)
            ml = mats[:, 0:KH * 16].rearrange("p (k e) -> p k e", k=KH)
            mr = mats[:, KH * 16:2 * KH * 16].rearrange("p (k e) -> p k e", k=KH)
            p4 = prod[:, :].rearrange("p (k e m) -> p k e m", k=KH, m=QC)
            for sgn, r0, dst in ((sgn_l, 0, ml), (sgn_r, 8, mr)):
                for k in range(KH):
                    V.tensor_tensor(p4[:, k], sgn[:, :].rearrange("p (e m) -> p e m", m=QC),
                                    q3[:, k, r0:r0 + 4].unsqueeze(1).to_broadcast([P, 16, QC]), ALU.mult)\
                        .then_inc(dve_chain, 1)
                count[0] += KH
                dve.wait_ge(dve_chain, count[0])
                link(V.tensor_reduce(dst, p4, AX.X, ALU.add))
            for k in range(KH):
                V.tensor_tensor(
                    prod[:, k * 64:(k + 1) * 64].rearrange("p (c d b) -> p c d b", c=QC, d=QC),
                    ml[:, k].rearrange("p (c b) -> p c b", c=QC).unsqueeze(2).to_broadcast([P, QC, QC, QC]),
                    mr[:, k].rearrange("p (b d) -> p d b", b=QC).unsqueeze(1).to_broadcast([P, QC, QC, QC]),
                    ALU.mult).then_inc(dve_chain, 1)
            count[0] += KH
            dve.wait_ge(dve_chain, count[0])
            link(V.tensor_reduce(r_full[:, :], prod[:, :].rearrange("p (e b) -> p e b", b=QC), AX.X, ALU.add))
            link(V.tensor_tensor(prod[:, 0:KH * 16].rearrange("p (e d) -> p e d", d=QC),
                                 r_full[:, :].rearrange("p (e d) -> p e d", d=QC),
                                 mask_c[:, :].unsqueeze(1).to_broadcast([P, KH * QC, QC]), ALU.mult))
            link(V.tensor_reduce(coef[:, :], prod[:, 0:KH * 16].rearrange("p (e d) -> p e d", d=QC), AX.X, ALU.add))
            dve.wait_ge(roots_ready, 1)
            link(V.reciprocal(nrm[:, 8:12], nrm[:, 4:8]))
            link(V.tensor_tensor(nrm[:, 8:12], nrm[:, 8:12], nrm[:, 0:4], ALU.mult))
            link(V.tensor_tensor(nrm[:, 8:12], nrm[:, 8:12], nrm[:, 4:8], ALU.add))
            link(V.tensor_scalar(nrm[:, 8:12], nrm[:, 8:12], 0.5, None, ALU.mult))
            link(V.reciprocal(nrm[:, 12:16], nrm[:, 8:12]))
            i3 = nrm[:, 12:16].rearrange("p (k s) -> p k s", k=KH)
            link(V.tensor_tensor(nrm[:, 0:2], i3[:, :, 0], i3[:, :, 1], ALU.mult))
            link(V.tensor_tensor(nrm[:, 0:2], nrm[:, 0:2], q3[:, :, 12], ALU.mult))
            c3 = coef[:, :].rearrange("p (k c) -> p k c", k=KH)
            link(V.tensor_tensor(c3, c3, nrm[:, 0:2].unsqueeze(2).to_broadcast([P, KH, QC]), ALU.mult))
            for k in range(KH):
                V.tensor_tensor(rot[:, k * P:(k + 1) * P].rearrange("p (c j) -> p c j", c=QC),
                                mask_j[:, :].unsqueeze(1).to_broadcast([P, QC, JH]),
                                c3[:, k].unsqueeze(2).to_broadcast([P, QC, JH]), ALU.mult).then_inc(rot_ready, 1)
            dve.wait_ge(rot_turned, 1)
            V.tensor_copy(rot_t[:, :], rt_ps[:, 0:KH * P]).then_inc(rot_t_ready, 1)
            for f in range(0, NB // 2, 2):
                if f == 4:
                    dve.wait_ge(wr_turned, 1)
                    V.tensor_copy(wr_rot[:, :], rt_ps[:, 256:256 + KH * NE]).then_inc(wr_ready, 1)
                dve.wait_ge(x_turned, f + 1)
                V.tensor_copy(arena_t[:, f * 512:(f + 1) * 512], pair[f % RING][:, :]).then_inc(x_t_even, 1)
            dve.wait_ge(b1_turned, 1)
            V.tensor_copy(b1_t[:, :], y_ps[:, 0:P])

            ne = "p (n e) -> p n e"
            lg3 = lg[:, :].rearrange(ne, n=NB)
            eq3 = eq[:, :].rearrange(ne, n=NB)
            rev3 = rev[:, :].unsqueeze(1).to_broadcast([P, NB, NE])
            dve.wait_ge(small_loaded, 48)
            dve.wait_ge(logits_ready, 1)
            dve.sem_inc(pair_free, RING)
            link(V.tensor_tensor(lg3, xt_ps[:, 0:NB * NE].rearrange(ne, n=NB),
                                 rb[:, :].unsqueeze(1).to_broadcast([P, NB, NE]), ALU.add))
            link(V.tensor_reduce(mx[:, :], lg3, AX.X, ALU.max))
            link(V.tensor_tensor(eq3, lg3, mx[:, :].unsqueeze(2).to_broadcast([P, NB, NE]), ALU.is_ge))
            link(V.tensor_tensor(eq3, eq3, rev3, ALU.mult))
            link(V.tensor_reduce(mx[:, :], eq3, AX.X, ALU.max))
            V.tensor_tensor(oh[:, :].rearrange("p (e n) -> p n e", n=NB), rev3,
                            mx[:, :].unsqueeze(2).to_broadcast([P, NB, NE]), ALU.is_equal).then_inc(oh_ready, 1)

            prefix = xr_ps[:, 0:P]
            totals = xr_ps[:, P:2 * P]
            gex3 = gex[:, :].rearrange("p (e n) -> p e n", n=NB)
            gin3 = gin[:, :].rearrange("p (e n) -> p e n", n=NB)
            cnt, til, tend, tst, off, zed = (sm[:, a * NE:(a + 1) * NE] for a in range(6))
            dve.wait_ge(ranks_ready, 1)
            link(V.tensor_tensor_scan(gin[:, :], ones[:, :], totals, 0.0, ALU.mult, ALU.add))
            link(V.tensor_tensor(gex[:, :], gin[:, :], totals, ALU.subtract))
            link(V.tensor_tensor(cnt, gin3[:, :, NB - 1], gex3[:, :, 0], ALU.subtract))
            over = ct[:, 0:NE * (TOK // ITEM - 1)].rearrange("p (e m) -> p e m", e=NE)
            link(V.scalar_tensor_tensor(over, cnt.unsqueeze(2).to_broadcast([P, NE, TOK // ITEM - 1]), 1.0 / ITEM,
                                        iota[:, 1:TOK // ITEM].unsqueeze(1).to_broadcast([P, NE, TOK // ITEM - 1]),
                                        ALU.mult, ALU.is_gt))
            link(V.tensor_reduce(til, over, AX.X, ALU.add))
            link(V.tensor_scalar(til, til, 1.0, None, ALU.add))
            link(V.tensor_tensor_scan(tend, ones[:, 0:NE], til, 0.0, ALU.mult, ALU.add))
            link(V.tensor_tensor(tst, tend, til, ALU.subtract))
            link(V.scalar_tensor_tensor(off, tst, float(ITEM), gex3[:, :, 0], ALU.mult, ALU.subtract))
            link(V.tensor_tensor(gex3, gex3, off.unsqueeze(2).to_broadcast([P, NE, NB]), ALU.add))
            link(V.tensor_tensor(pos[:, :], prefix, gex[:, :], ALU.add))
            link(V.tensor_tensor(pos[:, :], pos[:, :], oh[:, :], ALU.mult))
            link(V.tensor_reduce(mx[:, :], pos[:, :].rearrange("p (e n) -> p n e", n=NB), AX.X, ALU.add))
            link(V.tensor_copy(slot[:, :], mx[:, :]))
            link(V.tensor_single_scalar(slot_q[:, :], slot[:, :], 7, ALU.arith_shift_right))
            link(V.tensor_single_scalar(slot_r[:, :], slot[:, :], P - 1, ALU.bitwise_and))
            TS = TAB * NSUB
            V.tensor_tensor(slot_oh, iota[:, :].unsqueeze(1).to_broadcast([P, NB, P]),
                            slot_r[:, :].unsqueeze(2).to_broadcast([P, NB, P]), ALU.is_equal).then_inc(slots_ready, 1)
            q_oh3 = q_oh[:, :].rearrange("p (n q) -> p n q", n=NB)
            q_val4 = q_val[:, :].rearrange("p (n s q) -> p n s q", n=NB, s=2)
            link(V.tensor_tensor(q_oh3, iota[:, 0:TS].unsqueeze(1).to_broadcast([P, NB, TS]),
                                 slot_q[:, :].unsqueeze(2).to_broadcast([P, NB, TS]), ALU.is_equal))
            V.tensor_scalar(q_val4[:, :, 0, :], q_oh3, pcol[:, :], None, ALU.mult).then_inc(slots_ready, 1)
            V.tensor_tensor(q_val4[:, :, 1, :], q_oh3, iota[:, 0:NB].unsqueeze(2).to_broadcast([P, NB, TS]),
                            ALU.mult).then_inc(slots_ready, 1)

            def over_items(ap):
                return ap.unsqueeze(1).to_broadcast([P, TAB, NE])

            le_s, le_e, eq_s, tmp = (ct[:, a * TAB * NE:(a + 1) * TAB * NE].rearrange("p (i e) -> p i e", e=NE)
                                     for a in range(4))
            i_bc = iota[:, 0:TAB].unsqueeze(2).to_broadcast([P, TAB, NE])
            rem, steps, first, prep, expert, word, tmp3 = (cv[:, a * TAB:(a + 1) * TAB] for a in range(7))
            V.tensor_tensor(le_s, over_items(tst), i_bc, ALU.is_le)
            V.tensor_tensor(le_e, over_items(tend), i_bc, ALU.is_le)
            V.tensor_tensor(eq_s, over_items(tst), i_bc, ALU.is_equal)
            link(V.scalar_tensor_tensor(zed, tst, float(ITEM), cnt, ALU.mult, ALU.add))
            V.tensor_reduce(first, eq_s, AX.X, ALU.add)
            V.tensor_reduce(prep, eq_s[:, :, 0:NE - 1], AX.X, ALU.add)
            V.tensor_reduce(expert, le_e, AX.X, ALU.add)
            link(V.tensor_tensor(tmp, le_s, le_e, ALU.subtract))
            link(V.tensor_tensor(tmp, tmp, over_items(zed), ALU.mult))
            link(V.tensor_reduce(rem, tmp, AX.X, ALU.add))
            link(V.scalar_tensor_tensor(rem, rem, 1.0 / STEP, m4i[:, :], ALU.mult, ALU.add))
            tmp_s = ct[:, 0:TAB * (NSTEP - 1)].rearrange("p (i m) -> p i m", m=NSTEP - 1)
            link(V.tensor_tensor(tmp_s, rem.unsqueeze(2).to_broadcast([P, TAB, NSTEP - 1]),
                                 iota[:, 1:NSTEP].unsqueeze(1).to_broadcast([P, TAB, NSTEP - 1]), ALU.is_gt))
            V.tensor_reduce(steps, tmp_s, AX.X, ALU.add)
            link(V.tensor_scalar(expert, expert, float(NE - 1), 16.0, ALU.min, ALU.mult))
            link(V.scalar_tensor_tensor(word, first, 8.0, expert, ALU.mult, ALU.add))
            link(V.scalar_tensor_tensor(word, prep, 4.0, word, ALU.mult, ALU.add))
            V.memset(ctrl[:, 1:2], 0)
            V.tensor_scalar(ctrl[:, 0:1], tend[:, NE - 1:NE], -1.0, None, ALU.add)
            V.tensor_tensor(ctrl[:, 2:2 + TAB], word, steps, ALU.add).then_inc(ctrl_ready, 1)

            dve.wait_ge(idx_summed, 1)
            link(V.tensor_copy(idx_f[:, 0:2 * TS], y_ps[:, 0:2 * TS]))
            V.tensor_scalar(idx_f[:, 2 * TS:3 * TS], idx_f[:, 0:TS], 0.0, float(BIG), ALU.is_equal, ALU.mult)
            link(V.scalar_tensor_tensor(idx_f[:, 0:TS], idx_f[:, 0:TS], float(NB), idx_f[:, TS:2 * TS],
                                        ALU.mult, ALU.add))
            V.tensor_scalar(g_idx[:, :], idx_f[:, 0:TS], -float(NB), 0.0, ALU.add, ALU.max)
            V.scalar_tensor_tensor(s_idx[:, :], idx_f[:, 0:TS], -float(NB), idx_f[:, 2 * TS:3 * TS],
                                   ALU.add, ALU.add).then_inc(idx_ready, 1)

            def copy_xt(i):
                dve.wait_ge(xg_turned, i + 1)
                V.tensor_copy(xg_t[:, :], xt_ps[:, :]).then_inc(xg_t_done, 1)

            def split_x(i):
                dve.wait_ge(xr_hi_done, i + 1)
                here = bass.ds((i & 1) * (KH * ITEM), KH * ITEM)
                V.tensor_tensor(xr_lo[:, here], xr_ps[:, :], xr_hi[:, here].bitcast(F32), ALU.subtract)\
                    .then_inc(xr_lo_done, 1)

            dve.wait_ge(ctrl_ready, 1)
            last_item = load_last(dve)
            copy_xt(0)
            split_x(0)

            def gated(i, c, n):
                dve.wait_ge(sig_done, i * NC + (c + 1))
                V.scalar_tensor_tensor(u32[:, c, 0:n], pair[c % RING][:, 0:n], b1_cur[:, c:c + 1],
                                       sig[:, c % RING, 0:n], ALU.add, ALU.mult).then_inc(pair_free, 1)

            def lo_u(i, g, n):
                dve.wait_ge(u_hi_done, i * (NC // 2) + (g + 1))
                uv = [u[:, 2 * g * ITEM:(2 * g + 2) * ITEM].rearrange("p (c t) -> p c t", c=2)[:, :, 0:n]
                      for u in (u_lo, u_hi)]
                V.tensor_tensor(uv[0], u32[:, 2 * g:2 * g + 2, 0:n], uv[1].bitcast(F32), ALU.subtract)\
                    .then_inc(u_lo_done, 1)

            def lo_unit(parity, u, n_hi):
                dve.wait_ge(w1_hi_done, n_hi)
                V.tensor_tensor(w_lo[:, bass.ds(w_col(parity, u), UNIT)], w_raw[:, u * UNIT:(u + 1) * UNIT],
                                w_hi[:, bass.ds(w_col(parity, u), UNIT)].bitcast(F32), ALU.subtract)\
                    .then_inc(w1_split, 1)

            def add_rows(i, s_two):
                def rows(n):
                    dve.wait_ge(mm2_done, i + 1)
                    V.tensor_tensor(y_out[:, 0:n], y_ps[:, 0:n], xb[:, bass.ds((i & 3) * (NSUB * DIM), n)],
                                    ALU.add).then_inc(y_done, 1)

                with dve.If(s_two > 0):
                    rows(NSUB * DIM)
                with dve.Else():
                    rows(DIM)

            def item(i, word, n, prep, first=False):
                e = 0 if first else f_expert(word)
                dve.wait_ge(b1_cur_done, e + 1)
                for c in range(RING):
                    gated(i, c, n)
                    if prep and c < W1U:
                        lo_unit((e + 1) & 1, c, e * W1U + (W1U + c + 1))
                split_x(i + 1)
                if not first:
                    dve.wait_ge(xb_done, i + 2)
                    add_rows(i - 1, f_two(load_word(dve, i - 1)))
                lo_u(i, 0, n)
                lo_u(i, 1, n)
                for c in range(RING, NC):
                    gated(i, c, n)
                    if c % 2 == 1 and c > RING + 1:
                        lo_u(i, c // 2 - 1, n)
                lo_u(i, NC // 2 - 1, n)

            V.tensor_copy(b1_cur[:, :], b1_t[:, 0:2 * NC]).then_inc(b1_cur_done, 1)
            copy_xt(1)
            word = load_word(dve, 0)
            with dve.If(f_two(word) > 0):
                item(0, word, ITEM, True, first=True)
            with dve.Else():
                item(0, word, P, True, first=True)
            with dve.Fori(1, MAX_ITEMS) as i:
                with dve.If(i <= last_item):
                    word = load_word(dve, i)
                    with dve.If(f_first(word) > 0):
                        e = f_expert(word)
                        V.tensor_copy(b1_cur[:, :], b1_t[:, bass.ds(e * (2 * NC), 2 * NC)]).then_inc(b1_cur_done, 1)
                    copy_xt(i + 1)
                    with dve.If(f_prep(word) > 0):
                        with dve.If(f_two(word) > 0):
                            item(i, word, ITEM, True)
                        with dve.Else():
                            item(i, word, P, True)
                    with dve.Else():
                        with dve.If(f_two(word) > 0):
                            item(i, word, ITEM, False)
                        with dve.Else():
                            item(i, word, P, False)
            dve.wait_ge(scattered, last_item * (16 * NSUB))
            add_rows(last_item, f_two(load_word(dve, last_item)))

        @block.tensor
        def _(pe):
            T = nc.tensor
            pe.wait_ge(consts_ready, 5)
            pe.wait_ge(q_repeated, KH)
            for k in range(KH):
                last = T.matmul(rt_ps[:, k * 16:(k + 1) * 16], q_rep[:, k * P:(k + 1) * P], ident[0:13, 0:16],
                                start=True, stop=True)
            last.then_inc(q_spread, 1)

            def turn_x(f):
                if f >= RING:
                    if f % 2 == 0:
                        pe.wait_ge(x_t_even, (f - RING) // 2 + 1)
                    else:
                        pe.wait_ge(x_t_odd, (f - RING) // 2 + 1)
                pe.wait_ge(x_loaded[f // 2], 16)
                for a in range(2):
                    n = 2 * f + a
                    xk = x_tok[:, n, :].rearrange("p (m k) -> p k m", k=KH)
                    for k in range(KH):
                        last = T.transpose(pair[f % RING][:, (2 * a + k) * P:(2 * a + k + 1) * P], xk[:, k], ident[:, :])
                last.then_inc(x_turned, 1)

            for f in range(RING):
                turn_x(f)
            pe.wait_ge(rot_ready, KH)
            for k in range(KH):
                last = T.transpose(rt_ps[:, k * P:(k + 1) * P], rot[:, k * P:(k + 1) * P], ident[:, :])
            last.then_inc(rot_turned, 1)
            pe.wait_ge(small_loaded, 48)
            pe.wait_ge(rot_t_ready, 1)
            for k in range(KH):
                last = T.matmul(rt_ps[:, 256 + k * NE:256 + (k + 1) * NE], rot_t[:, k * P:(k + 1) * P],
                                wr[:, k * NE:(k + 1) * NE], start=True, stop=True)
            last.then_inc(wr_turned, 1)
            T.transpose(y_ps[:, 0:P], b1_rows[:, :], ident[:, :]).then_inc(b1_turned, 1)
            for f in range(RING, NB // 2):
                turn_x(f)
            pe.wait_ge(wr_ready, 1)
            pe.wait_ge(x_t_even, NB // 4)
            pe.wait_ge(x_t_odd, NB // 4)
            for n in range(NB):
                for k in range(KH):
                    last = T.matmul(xt_ps[:, n * NE:(n + 1) * NE], x_t[:, n, k, :], wr_rot[:, k * NE:(k + 1) * NE],
                                    start=(k == 0), stop=(k == KH - 1))
            last.then_inc(logits_ready, 1)
            pe.wait_ge(oh_ready, 1)
            T.matmul(xr_ps[:, 0:P], lower[:, :], oh[:, :], start=True, stop=True)
            T.matmul(xr_ps[:, P:2 * P], ones16[:, :], oh[:, :], start=True, stop=True).then_inc(ranks_ready, 1)
            TS = TAB * NSUB
            pe.wait_ge(slots_ready, 3)
            for n in range(NB):
                last = T.matmul(y_ps[:, 0:2 * TS], slot_oh[:, n, :], q_val[:, n * 2 * TS:(n + 1) * 2 * TS],
                                start=(n == 0), stop=(n == NB - 1))
            last.then_inc(idx_summed, 1)

            def turn_item(i):
                pe.wait_ge(gathered, i * (16 * NSUB) + 16 * NSUB)
                if not (isinstance(i, int) and i == 0):
                    pe.wait_ge(xg_t_done, i)
                for k in range(KH):
                    for s in range(NSUB):
                        xk = xg[:, s * DIM:(s + 1) * DIM].rearrange("p (m k) -> p k m", k=KH)
                        last = T.transpose(xt_ps[:, k * ITEM + s * P:k * ITEM + (s + 1) * P], xk[:, k], ident[:, :])
                last.then_inc(xg_turned, 1)

            def rotate(i):
                pe.wait_ge(xg_t_done, i + 1)
                if not (isinstance(i, int) and i == 0):
                    pe.wait_ge(xr_lo_done, i)
                for k in range(KH):
                    last = T.matmul(xr_ps[:, k * ITEM:(k + 1) * ITEM], rot[:, k * P:(k + 1) * P],
                                    xg_t[:, k * ITEM:(k + 1) * ITEM], start=True, stop=True)
                last.then_inc(rotated, 1)

            pe.wait_ge(idx_ready, 1)
            turn_item(0)
            rotate(0)
            pe.wait_ge(ctrl_ready, 1)
            last_item = load_last(pe)

            def first_product(i, e, parity, steps, chunks):
                n = steps * STEP
                x_at = (i & 1) * (KH * ITEM)
                for c in chunks:
                    if c == 0:
                        pe.wait_ge(xr_lo_done, i + 1)
                    if c % 2 == 0:
                        pe.wait_ge(w1_split, e * W1U + (c // 2 + 1))
                    pe.wait_ge(pair_free, i * NC + (c + 1))
                    for ag in range(2):
                        dst = pair[c % RING][:, ag * ITEM:ag * ITEM + n]
                        for k in range(KH):
                            at = w_col(parity, c // 2) + k * 512 + ag * 256 + (c % 2) * P
                            xh = xr_hi[:, bass.ds(x_at + k * ITEM, n)]
                            xl = xr_lo[:, bass.ds(x_at + k * ITEM, n)]
                            T.matmul(dst, w_hi[:, at:at + P], xh, start=(k == 0), stop=False)
                            T.matmul(dst, w_hi[:, at:at + P], xl, start=False, stop=False)
                            last = T.matmul(dst, w_lo[:, at:at + P], xh, start=False, stop=(k == KH - 1))
                    last.then_inc(mm1_done, 1)

            def by_size(i, word, chunks, first=False):
                e = 0 if first else f_expert(word)
                steps = f_steps(word)

                def sizes(parity):
                    with pe.If(steps < 2):
                        with pe.If(steps < 1):
                            first_product(i, e, parity, 1, chunks)
                        with pe.Else():
                            first_product(i, e, parity, 2, chunks)
                    with pe.Else():
                        with pe.If(steps < 3):
                            first_product(i, e, parity, 3, chunks)
                        with pe.Else():
                            first_product(i, e, parity, 4, chunks)

                if first:
                    sizes(0)
                    return
                with pe.If((e & 1) < 1):
                    sizes(0)
                with pe.Else():
                    sizes(1)

            def second_product(i, word):
                e = f_expert(word)
                w_at = (e & 1) * (WU * UNIT)

                def block_of_tokens(s, last_block):
                    for c in range(NC):
                        if s == 0 and c % CPU2 == 0:
                            pe.wait_ge(w2_split, e * W2U + (c // CPU2 + 1))
                        if s == 0 and c % 2 == 0:
                            pe.wait_ge(u_lo_done, i * (NC // 2) + (c // 2 + 1))
                        wv = bass.ds(w_at + (W1U + c // CPU2) * UNIT + (c % CPU2) * DIM, DIM)
                        uv = slice(c * ITEM + s * P, c * ITEM + (s + 1) * P)
                        dst = y_ps[:, s * DIM:(s + 1) * DIM]
                        T.matmul(dst, u_hi[:, uv], w_hi[:, wv], start=(c == 0), stop=False)
                        T.matmul(dst, u_hi[:, uv], w_lo[:, wv], start=False, stop=False)
                        last = T.matmul(dst, u_lo[:, uv], w_hi[:, wv], start=False, stop=(c == NC - 1))
                    if last_block:
                        last.then_inc(mm2_done, 1)

                with pe.If(f_two(word) > 0):
                    block_of_tokens(0, False)
                    block_of_tokens(1, True)
                with pe.Else():
                    block_of_tokens(0, True)

            word = load_word(pe, 0)
            turn_item(1)
            by_size(0, word, range(0, RING), first=True)
            rotate(1)
            by_size(0, word, range(RING, NC), first=True)
            with pe.Fori(1, MAX_ITEMS) as i:
                with pe.If(i <= last_item):
                    word = load_word(pe, i)
                    turn_item(i + 1)
                    by_size(i, word, range(0, RING))
                    rotate(i + 1)
                    second_product(i - 1, load_word(pe, i - 1))
                    by_size(i, word, range(RING, NC))
            second_product(last_item, load_word(pe, last_item))


_INS = ['x', 'cond_256', 'L0_cond_q_right', 'L0_cond_spectral_gate', 'L0_ffn_router_w', 'L0_ffn_router_b',
        'L0_ffn_w1', 'L0_ffn_b1', 'L0_ffn_w2', 'L0_ffn_b2']
_OUTS = [((8, 256, 256), 'float32')]


def kernel(**inputs):
    import numpy as _np
    import concourse.bacc as _bacc
    from concourse import mybir as _mybir
    from concourse.bass_utils import run_bass_kernel_spmd as _run

    nc = _bacc.Bacc("TRN2", target_bir_lowering=False, num_devices=1)
    arrays, args = {}, []
    for name in _INS:
        a = _np.ascontiguousarray(inputs[name])
        arrays[f"in_{name}_dram"] = a
        args.append(nc.dram_tensor(f"in_{name}_dram", a.shape, _mybir.dt.from_np(a.dtype), kind="ExternalInput").ap())
    for i, (shape, dtype) in enumerate(_OUTS):
        dt = _mybir.dt.from_np(_np.dtype(dtype))
        args.append(nc.dram_tensor(f"out_{i}_dram", shape, dt, kind="ExternalOutput").ap())
    adaln_moe_ffn_kernel(nc, *args)
    r = _run(nc, [arrays], core_ids=[0])
    got = tuple(r.results[0][f"out_{i}_dram"] for i in range(len(_OUTS)))
    return got[0]
```

```python
import concourse.bass as bass
from concourse import mybir
from contextlib import ExitStack


def adaln_moe_ffn_kernel(nc, x, cond, q_right, gate, router_w, router_b, w1, b1, w2, b2, out):
    F32 = mybir.dt.float32
    F32R = mybir.dt.float32r
    BF16 = mybir.dt.bfloat16
    I32 = mybir.dt.int32
    U32 = mybir.dt.uint32
    ALU = mybir.AluOpType
    ACT = mybir.ActivationFunctionType
    AX = mybir.AxisListType

    P = 128
    BATCH, SEQ, DIM = x.shape
    TOK = BATCH * SEQ
    NB = TOK // P
    NE = router_w.shape[1]
    HID = w2.shape[1]
    QC = 4
    QD = DIM // QC
    KH = DIM // P
    JH = QD // KH
    NC = HID // P
    ITEM = 512
    NSUB = ITEM // P
    STEP = 64
    NSTEP = ITEM // STEP
    MIN_STEPS = 4
    MAX_ITEMS = TOK // ITEM + NE - 1
    TAB = MAX_ITEMS + 3
    UNIT = 1024
    W1U = KH * 2 * HID // UNIT
    W2U = HID // P * DIM // UNIT
    WU = W1U + W2U
    CPU2 = UNIT // DIM
    PIECE = UNIT // 2
    W1P = W1U * UNIT // PIECE
    W2P = W2U * UNIT // PIECE
    RING = 2
    U_RING = 4
    LAG = 3
    TURN = 4
    BIG = 4096
    EPS = 1e-8

    x_flat = x.rearrange("b s d -> (b s) d")
    out_flat = out.rearrange("b s d -> (b s) d")

    ctx = ExitStack()
    with ctx:
        def sb(name, cols, dt=F32, rows=P):
            return ctx.enter_context(nc.sbuf_tensor(name, [rows, cols], dt))

        def ps(name):
            return ctx.enter_context(nc.psum_tensor(name, [P, 512], F32))

        def sem(name):
            return ctx.enter_context(nc.semaphore(name))

        w_raw = sb("w_raw", WU * UNIT)
        w_hi = sb("w_hi", 2 * WU * UNIT, F32R)
        w_lo = sb("w_lo", 2 * WU * UNIT, F32R)
        arena = sb("arena", NB * DIM)
        x_tok = arena[:, :].rearrange("p (n d) -> p n d", n=NB)
        u32 = arena[:, 0:U_RING * ITEM].rearrange("p (c t) -> p c t", c=U_RING)
        sig = arena[:, U_RING * ITEM:(U_RING + RING) * ITEM].rearrange("p (c t) -> p c t", c=RING)
        arena_t = sb("arena_t", NB * DIM)
        x_t = arena_t[:, :].rearrange("p (k t) -> p k t", k=KH)
        xb = arena_t[:, 0:2 * NSUB * DIM]
        u_hi = sb("u_hi", U_RING * ITEM, F32R)
        u_lo = sb("u_lo", U_RING * ITEM, F32R)
        xr_hi = sb("xr_hi", KH * ITEM, F32R)
        xr_lo = sb("xr_lo", KH * ITEM, F32R)
        x_item = sb("x_item", NSUB * DIM + KH * ITEM)
        xg = x_item[:, 0:NSUB * DIM]
        xg_t = x_item[:, NSUB * DIM:NSUB * DIM + KH * ITEM]
        logits_t = x_item[0:NE, 0:TOK]
        y_out = sb("y_out", NSUB * DIM)
        b1_rows = sb("b1_rows", P)
        b1_t = sb("b1_t", P)
        b1_cur = sb("b1_cur", 2 * NC)
        b2_all = sb("b2_all", NE * DIM)
        g_cur = sb("g_cur", NSUB, I32)
        s_cur = sb("s_cur", NSUB, I32)
        g_idx = sb("g_idx", TAB * NSUB, I32)
        s_idx = sb("s_idx", TAB * NSUB, I32)
        ctrl = sb("ctrl", 1 + TAB, I32)
        ident = sb("ident", P)
        iota = sb("iota", P)
        lower = sb("lower", P, BF16)
        ones16 = sb("ones16", P, BF16)
        ones = sb("ones", P)
        zeros16 = sb("zeros16", 2 * DIM, BF16, rows=1)
        pcol = sb("pcol", 1)
        rev = sb("rev", NE)
        m4i = sb("m4i", TAB)
        sgn_l = sb("sgn_l", 64)
        sgn_r = sb("sgn_r", 64)
        mask_j = sb("mask_j", JH)
        mask_c = sb("mask_c", QC)
        q_rows = sb("q_rows", QD, rows=13)
        q_rep = sb("q_rep", KH * P, rows=13)
        qv = sb("qv", KH * 16)
        qsq = sb("qsq", KH * 16)
        nrm = sb("nrm", 4 * KH * 2)
        mats = sb("mats", 2 * KH * 16)
        prod = sb("prod", KH * 64)
        r_full = sb("r_full", KH * 16)
        coef = sb("coef", KH * QC)
        coef_t = sb("coef_t", KH * QC)
        rot = sb("rot", KH * P)
        rot_t = sb("rot_t", KH * P)
        iota16 = sb("iota16", P, BF16)
        wr = sb("wr", KH * NE)
        wr_rot = sb("wr_rot", KH * NE)
        rb = sb("rb", NE)
        mx = sb("mx", NB)
        oh = sb("oh", NB * NE, BF16)
        sm = sb("sm", 8 * NE)
        slot = sb("slot", NB, I32)
        slot_q = sb("slot_q", NB, I32)
        slot_r = sb("slot_r", NB, I32)
        idx_f = sb("idx_f", 3 * TAB * NSUB)

        def part(a, at, cols):
            return a[:, at:at + cols]

        ct = part(arena, 0, 4 * TAB * NE)
        cv = part(arena, 4 * TAB * NE, 8 * TAB)
        q_oh = part(arena, 4 * TAB * NE + 8 * TAB, NB * TAB * NSUB // 2).bitcast(BF16)
        lg, eq, gin, gex, pos = (part(arena, NB * DIM - (a + 1) * NB * NE, NB * NE) for a in range(5))
        slot_oh = part(arena_t, 2 * NSUB * DIM, NB * P // 2).bitcast(BF16).rearrange("p (n r) -> p n r", n=NB)
        q_val = part(arena_t, 2 * NSUB * DIM + NB * P // 2, NB * TAB * NSUB).bitcast(BF16)

        pair = [[ps(f"{ag}{b}_ps") for ag in "ag"] for b in range(RING)]
        y_ps = [ps(f"y{h}_ps") for h in range(2)]
        xk_ps = [ps(f"xk{k}_ps") for k in range(KH)]
        turn_ps = pair[0] + pair[1]
        early_ps, late_ps = y_ps

        consts_ready = sem("consts_ready")
        pool_chain = sem("pool_chain")
        dve_chain = sem("dve_chain")
        q_loaded = sem("q_loaded")
        small_loaded = sem("small_loaded")
        b2_loaded = sem("b2_loaded")
        x_loaded = [sem(f"x_loaded{g}") for g in range(4)]
        w_loaded = [sem(f"w_loaded{u}") for u in range(WU)]
        q_repeated = sem("q_repeated")
        q_spread = sem("q_spread")
        sums_ready = sem("sums_ready")
        roots_ready = sem("roots_ready")
        rot_ready = sem("rot_ready")
        rot_t_ready = sem("rot_t_ready")
        wr_turned = sem("wr_turned")
        wr_ready = sem("wr_ready")
        b1_turned = sem("b1_turned")
        b1_t_done = sem("b1_t_done")
        x_turned = sem("x_turned")
        x_t_done = sem("x_t_done")
        logits_t_ready = sem("logits_t_ready")
        logits_t_done = sem("logits_t_done")
        logits_ready = sem("logits_ready")
        oh_ready = sem("oh_ready")
        ranks_ready = sem("ranks_ready")
        slots_ready = sem("slots_ready")
        idx_summed = sem("idx_summed")
        ctrl_ready = sem("ctrl_ready")
        idx_ready = sem("idx_ready")
        w1_hi_done = sem("w1_hi_done")
        w2_hi_done = sem("w2_hi_done")
        w1_first_split = sem("w1_first_split")
        w1_split = sem("w1_split")
        w2_split = sem("w2_split")
        gathered = sem("gathered")
        scattered = sem("scattered")
        xb_done = sem("xb_done")
        xg_turned = sem("xg_turned")
        xg_t_done = sem("xg_t_done")
        rotated = sem("rotated")
        xr_hi_done = sem("xr_hi_done")
        xr_lo_done = sem("xr_lo_done")
        b1_cur_done = sem("b1_cur_done")
        mm1_done = sem("mm1_done")
        sig_done = sem("sig_done")
        pair_free = sem("pair_free")
        u_hi_done = sem("u_hi_done")
        u_lo_done = sem("u_lo_done")
        mm2_done = sem("mm2_done")
        y_done = sem("y_done")

        block = ctx.enter_context(nc.Block())

        def w_col(parity, unit):
            return parity * (WU * UNIT) + unit * UNIT

        def f_steps(w):
            return w & 7

        def f_blocks(w):
            return ((w & 7) + 1) >> 1

        def f_prep(w):
            return (w >> 3) & 1

        def f_first(w):
            return (w >> 4) & 1

        def f_expert(w):
            return (w >> 5).with_bounds(min_val=0, max_val=NE - 1)

        def load_last(eng):
            return eng.value_load(ctrl[0:1, 0:1], min_val=NE - 1, max_val=MAX_ITEMS - 1)

        def load_word(eng, i):
            return eng.value_load(ctrl[0:1, bass.ds(i + 1, 1)], min_val=0, max_val=255)

        @block.sync
        def _(sp):
            sp.dma_start(q_rows[0:8, :], cond).then_inc(q_loaded, 16)
            xv = x_flat.rearrange("(p n) d -> p n d", p=P)
            for g in range(4):
                sp.dma_start(x_tok[:, 4 * g:4 * g + 4, :], xv[:, 4 * g:4 * g + 4, :]).then_inc(x_loaded[g], 16)

            w1_v = w1.rearrange("e (m k) (ag f) -> e m (k ag) f", k=KH, ag=2)
            w2_v = w2.rearrange("e (h c p) d -> e h p c d", h=W2U, p=P)

            def load_unit(e, u):
                if u < W1U:
                    dst = w_raw[:, u * UNIT:(u + 1) * UNIT].rearrange("p (b f) -> p b f", b=2 * KH)
                    sp.dma_start(dst, w1_v[e, :, :, u * 256:(u + 1) * 256]).then_inc(w_loaded[u], 16)
                else:
                    dst = w_raw[:, u * UNIT:(u + 1) * UNIT].rearrange("p (c d) -> p c d", d=DIM)
                    sp.dma_start(dst, w2_v[e, u - W1U]).then_inc(w_loaded[u], 16)

            for u in range(WU):
                load_unit(0, u)
            sp.dma_start(b2_all[:, :], b2.rearrange("e d -> (e d)").partition_broadcast(P)).then_inc(b2_loaded, 16)
            with sp.Fori(1, NE) as e:
                for u in range(WU):
                    if u < W1U:
                        sp.wait_ge(w1_split, e * W1P - (W1P - 2 * u - 2))
                    else:
                        sp.wait_ge(w2_split, e * W2U - (W2U - (u - W1U) - 1))
                    load_unit(e, u)

        @block.gpsimd
        def _(pool):
            count = [0]

            def link(ins):
                count[0] += 1
                ins.then_inc(pool_chain, 1)
                pool.wait_ge(pool_chain, count[0])

            nc.gpsimd.memset(ones[:, :], 1.0).then_inc(pool_chain, 1)
            nc.gpsimd.memset(ones16[:, :], 1.0).then_inc(pool_chain, 1)
            nc.gpsimd.memset(sgn_l[:, :], 0.0).then_inc(pool_chain, 1)
            nc.gpsimd.memset(sgn_r[:, :], 0.0).then_inc(pool_chain, 1)
            nc.gpsimd.memset(y_out[:, :], 0.0).then_inc(pool_chain, 1)
            nc.gpsimd.memset(zeros16[:, :], 0.0).then_inc(pool_chain, 1)
            count[0] = 6
            pool.wait_ge(pool_chain, count[0])
            nc.gpsimd.affine_select(out=ident[:, :], in_=ones[:, :], compare_op=ALU.is_equal, fill=0.0,
                                    base=0, pattern=[[-1, P]], channel_multiplier=1).then_inc(consts_ready, 1)
            left = ((1, -1, -1, -1), (1, 1, -1, 1), (1, 1, 1, -1), (1, -1, 1, 1))
            right = ((1, -1, -1, -1), (1, 1, 1, -1), (1, -1, 1, 1), (1, 1, -1, 1))
            for a in range(QC):
                for b in range(QC):
                    m = a ^ b
                    conj = 1 if m == 0 else -1
                    nc.gpsimd.memset(sgn_l[:, a * 16 + b * 4 + m:a * 16 + b * 4 + m + 1], float(left[a][b]))
                    last = nc.gpsimd.memset(sgn_r[:, a * 16 + b * 4 + m:a * 16 + b * 4 + m + 1],
                                            float(right[a][b] * conj))
            last.then_inc(consts_ready, 1)
            nc.gpsimd.iota(iota[:, :], pattern=[[1, P]], base=0, channel_multiplier=0,
                           allow_small_or_imprecise_dtypes=True).then_inc(consts_ready, 1)
            nc.gpsimd.iota(iota16[:, :], pattern=[[1, P]], base=0, channel_multiplier=0,
                           allow_small_or_imprecise_dtypes=True).then_inc(consts_ready, 1)
            nc.gpsimd.iota(pcol[:, :], pattern=[[0, 1]], base=1, channel_multiplier=1,
                           allow_small_or_imprecise_dtypes=True).then_inc(consts_ready, 1)
            nc.gpsimd.affine_select(out=lower[:, :], in_=ones16[:, :], compare_op=ALU.is_ge, fill=0.0,
                                    base=-1, pattern=[[1, P]], channel_multiplier=-1).then_inc(consts_ready, 1)

            def lo_unit(parity, u, done, hi_done, n_hi):
                pool.wait_ge(hi_done, n_hi)
                nc.gpsimd.tensor_tensor(w_lo[:, bass.ds(w_col(parity, u), UNIT)],
                                        w_raw[:, u * UNIT:(u + 1) * UNIT],
                                        w_hi[:, bass.ds(w_col(parity, u), UNIT)].bitcast(F32),
                                        ALU.subtract).then_inc(done, 1)

            for u in range(W1U):
                lo_unit(0, u, w1_first_split, w1_hi_done, 2 * u + 2)

            pool.wait_ge(idx_ready, 1)
            pool.wait_ge(ctrl_ready, 1)
            last_item = load_last(pool)

            row_bound = pool.to_reg(TOK - 1)

            def issue_gather(idx):
                for s in range(NSUB):
                    nc.gpsimd.indirect_dma_start(
                        out=xg[:, s * DIM:(s + 1) * DIM], out_offset=None, in_=x_flat,
                        in_offset=bass.IndirectOffsetOnAxis(ap=idx[:, s:s + 1], axis=0),
                        bounds_check=row_bound, oob_is_err=False).then_inc(gathered, 16)

            def add_b2(i, word):
                e = f_expert(word)
                dst = xb[:, bass.ds((i & 1) * (NSUB * DIM), NSUB * DIM)]
                nc.gpsimd.tensor_tensor(
                    dst.rearrange("p (s d) -> p s d", s=NSUB),
                    xg[:, :].rearrange("p (s d) -> p s d", s=NSUB),
                    b2_all[:, bass.ds(e * DIM, DIM)].unsqueeze(1).to_broadcast([P, NSUB, DIM]),
                    ALU.add).then_inc(xb_done, 1)

            issue_gather(g_idx[:, 0:NSUB])
            pool.wait_ge(b2_loaded, 16)
            pool.wait_ge(gathered, 16 * NSUB)
            add_b2(0, load_word(pool, 0))
            pool.wait_ge(xb_done, 1)
            pool.wait_ge(xg_turned, KH)
            issue_gather(g_idx[:, NSUB:2 * NSUB])
            for u in range(W2U):
                lo_unit(0, W1U + u, w2_split, w2_hi_done, 2 * u + 2)

            base = count[0]

            def item(i, first=False):
                word = load_word(pool, i)
                if not first:
                    pool.wait_ge(scattered, i * (16 * NSUB))
                pool.wait_ge(gathered, i * (16 * NSUB) + 32 * NSUB)
                add_b2(i + 1, load_word(pool, i + 1))
                pool.wait_ge(xb_done, i + 2)
                pool.wait_ge(xg_turned, i * KH + 2 * KH)
                nc.gpsimd.tensor_copy(g_cur[:, :], g_idx[:, bass.ds(i * NSUB + 2 * NSUB, NSUB)])\
                    .then_inc(pool_chain, 1)
                step = pool.to_reg(i * 2 + (base + 1))
                pool.wait_ge(idx_ready, 1)
                pool.wait_ge(pool_chain, step)
                issue_gather(g_cur)
                with pool.If(f_prep(word) > 0):
                    e = f_expert(word)
                    for u in range(W2U):
                        lo_unit((e + 1) & 1, W1U + u, w2_split, w2_hi_done, e * W2P + (W2P + 2 * u + 2))
                pool.wait_ge(y_done, i * 2 + 2)
                nc.gpsimd.tensor_copy(s_cur[:, :], s_idx[:, bass.ds(i * NSUB, NSUB)]).then_inc(pool_chain, 1)
                step = pool.to_reg(i * 2 + (base + 2))
                pool.wait_ge(idx_ready, 1)
                pool.wait_ge(pool_chain, step)
                for s in range(NSUB):
                    nc.gpsimd.indirect_dma_start(
                        out=out_flat, out_offset=bass.IndirectOffsetOnAxis(ap=s_cur[:, s:s + 1], axis=0),
                        in_=y_out[:, s * DIM:(s + 1) * DIM], in_offset=None,
                        bounds_check=row_bound, oob_is_err=False).then_inc(scattered, 16)

            item(0, first=True)
            with pool.Fori(1, MAX_ITEMS) as i:
                with pool.If(i <= last_item):
                    item(i)
            pool.wait_ge(scattered, last_item * (16 * NSUB) + 16 * NSUB)
            pool.wait_ge(gathered, last_item * (16 * NSUB) + 48 * NSUB)

        @block.scalar
        def _(act):
            act.dma_start(q_rows[8:12, :], q_right).then_inc(q_loaded, 16)
            act.dma_start(q_rows[12:13, :], gate.rearrange("a b c j -> (a b c) j")).then_inc(q_loaded, 16)
            act.dma_start(wr[:, :], router_w.rearrange("(m k) e -> m (k e)", k=KH)).then_inc(small_loaded, 16)
            act.dma_start(rb[:, :], router_b.partition_broadcast(P)).then_inc(small_loaded, 16)
            act.dma_start(b1_rows[:, :], b1.rearrange("e (c f) -> (e c) f", f=P)).then_inc(small_loaded, 16)

            for f in range(NB // 2):
                if f == 2:
                    act.wait_ge(sums_ready, 1)
                    nc.scalar.activation(nrm[:, 4:8], nrm[:, 0:4], ACT.Sqrt).then_inc(roots_ready, 1)
                act.wait_ge(x_turned, f + 1)
                nc.scalar.activation(x_t[:, f % 2, (f // 2) * 512:(f // 2 + 1) * 512], turn_ps[f % 4][:, :], ACT.Copy)\
                    .then_inc(x_t_done, 1)
            act.wait_ge(b1_turned, 1)
            nc.scalar.activation(b1_t[:, :], early_ps[:, 0:P], ACT.Copy).then_inc(b1_t_done, 1)
            for g in range(4):
                act.wait_ge(logits_t_ready, g + 1)
                nc.scalar.activation(logits_t[:, g * 512:(g + 1) * 512], xk_ps[g % 2][0:NE, :], ACT.Copy)\
                    .then_inc(logits_t_done, 1)

            def hi_part(parity, at, cols, n_loaded):
                u = at // UNIT
                act.wait_ge(w_loaded[u], n_loaded)
                nc.scalar.activation(w_hi[:, bass.ds(w_col(parity, 0) + at, cols)], w_raw[:, at:at + cols], ACT.Copy)\
                    .then_inc(w1_hi_done if u < W1U else w2_hi_done, cols // PIECE)

            for u in range(WU):
                hi_part(0, u * UNIT, UNIT, 16)

            def split_x(i):
                for k in range(KH):
                    act.wait_ge(rotated, i * KH + (k + 1))
                    nc.scalar.activation(xr_hi[:, k * ITEM:(k + 1) * ITEM], xk_ps[k][:, :], ACT.Copy)\
                        .then_inc(xr_hi_done, 1)

            split_x(0)
            act.wait_ge(ctrl_ready, 1)
            last_item = load_last(act)

            def gates(i, c, n):
                act.wait_ge(mm1_done, i * NC + (c + 1))
                nc.scalar.activation(sig[:, c % RING, 0:n], pair[c % RING][1][:, 0:n], ACT.Sigmoid,
                                     bias=b1_cur[:, NC + c:NC + c + 1]).then_inc(sig_done, 1)

            def hi_u(i, c, n):
                act.wait_ge(pair_free, i * NC + (RING + c + 1))
                at = (c % U_RING) * ITEM
                nc.scalar.activation(u_hi[:, at:at + n], u32[:, c % U_RING, 0:n], ACT.Copy).then_inc(u_hi_done, 1)

            def item(i, word, n, prep):
                e = f_expert(word)
                act.wait_ge(b1_cur_done, e + 1)
                for c in range(NC):
                    gates(i, c, n)
                    if c > 0:
                        hi_u(i, c - 1, n)
                    if prep:
                        hi_part((e + 1) & 1, c * PIECE, PIECE, e * 16 + 32)
                        if c < W2P:
                            hi_part((e + 1) & 1, (W1P + c) * PIECE, PIECE, e * 16 + 32)
                hi_u(i, NC - 1, n)
                split_x(i + 1)

            with act.Fori(0, MAX_ITEMS) as i:
                with act.If(i <= last_item):
                    word = load_word(act, i)
                    blocks = f_blocks(word)
                    with act.If(f_prep(word) > 0):
                        with act.If(blocks < 1):
                            item(i, word, 2 * P, True)
                        with act.Else():
                            with act.If(blocks < 2):
                                item(i, word, 3 * P, True)
                            with act.Else():
                                item(i, word, 4 * P, True)
                    with act.Else():
                        with act.If(blocks < 1):
                            item(i, word, 2 * P, False)
                        with act.Else():
                            with act.If(blocks < 2):
                                item(i, word, 3 * P, False)
                            with act.Else():
                                item(i, word, 4 * P, False)

        @block.vector
        def _(dve):
            count = [0]

            def link(ins):
                count[0] += 1
                ins.then_inc(dve_chain, 1)
                dve.wait_ge(dve_chain, count[0])

            V = nc.vector
            dve.wait_ge(q_loaded, 48)
            for k in range(KH):
                V.tensor_copy(q_rep[:, k * P:(k + 1) * P].rearrange("r (c j) -> r c j", c=QC),
                              q_rows[:, :].rearrange("r (j k) -> r k j", k=KH)[:, k].unsqueeze(1)
                              .to_broadcast([13, QC, JH])).then_inc(q_repeated, 1)
            dve.wait_ge(consts_ready, 6)
            V.tensor_reduce(mask_j[:, :], ident[:, :].rearrange("p (c j) -> p j c", c=QC), AX.X, ALU.add)
            V.tensor_reduce(mask_c[:, :], ident[:, :].rearrange("p (c j) -> p c j", c=QC), AX.X, ALU.add)
            V.tensor_scalar(rev[:, :], iota[:, 0:NE], -1.0, float(NE), ALU.mult, ALU.add)
            V.tensor_scalar(m4i[:, :], iota[:, 0:TAB], -float(NSTEP), None, ALU.mult)
            dve.wait_ge(q_spread, 1)
            link(V.tensor_copy(qv[:, :], late_ps[:, 0:KH * 16]))
            q3 = qv[:, :].rearrange("p (k r) -> p k r", k=KH)
            s3 = qsq[:, :].rearrange("p (k r) -> p k r", k=KH)
            link(V.tensor_tensor(qsq[:, :], qv[:, :], qv[:, :], ALU.mult))
            n3 = nrm[:, 0:4].rearrange("p (k s) -> p k s", k=KH)
            V.tensor_reduce(n3[:, :, 0], s3[:, :, 0:8], AX.X, ALU.add)
            link(V.tensor_reduce(n3[:, :, 1], s3[:, :, 8:12], AX.X, ALU.add))
            V.tensor_scalar(nrm[:, 0:4], nrm[:, 0:4], EPS, None, ALU.add).then_inc(sums_ready, 1)
            ml = mats[:, 0:KH * 16].rearrange("p (k e) -> p k e", k=KH)
            mr = mats[:, KH * 16:2 * KH * 16].rearrange("p (k e) -> p k e", k=KH)
            p4 = prod[:, :].rearrange("p (k e m) -> p k e m", k=KH, m=QC)
            for sgn, r0, dst in ((sgn_l, 0, ml), (sgn_r, 8, mr)):
                for k in range(KH):
                    V.tensor_tensor(p4[:, k], sgn[:, :].rearrange("p (e m) -> p e m", m=QC),
                                    q3[:, k, r0:r0 + 4].unsqueeze(1).to_broadcast([P, 16, QC]), ALU.mult)\
                        .then_inc(dve_chain, 1)
                count[0] += KH
                dve.wait_ge(dve_chain, count[0])
                link(V.tensor_reduce(dst, p4, AX.X, ALU.add))
            for k in range(KH):
                V.tensor_tensor(
                    prod[:, k * 64:(k + 1) * 64].rearrange("p (c d b) -> p c d b", c=QC, d=QC),
                    ml[:, k].rearrange("p (c b) -> p c b", c=QC).unsqueeze(2).to_broadcast([P, QC, QC, QC]),
                    mr[:, k].rearrange("p (b d) -> p d b", b=QC).unsqueeze(1).to_broadcast([P, QC, QC, QC]),
                    ALU.mult).then_inc(dve_chain, 1)
            count[0] += KH
            dve.wait_ge(dve_chain, count[0])
            link(V.tensor_reduce(r_full[:, :], prod[:, :].rearrange("p (e b) -> p e b", b=QC), AX.X, ALU.add))
            r4 = r_full[:, :].rearrange("p (k c d) -> p k c d", k=KH, c=QC)
            mc = mask_c[:, :].unsqueeze(1).to_broadcast([P, QC, QC])
            pt = prod[:, 0:KH * 16].rearrange("p (k d c) -> p k d c", k=KH, d=QC)
            pc = prod[:, KH * 16:2 * KH * 16].rearrange("p (k c d) -> p k c d", k=KH, c=QC)
            for k in range(KH):
                V.tensor_tensor(pt[:, k], r4[:, k].rearrange("p c d -> p d c"), mc, ALU.mult)
                last = V.tensor_tensor(pc[:, k], r4[:, k], mc, ALU.mult)
            link(last)
            V.tensor_reduce(coef_t[:, :], pt.rearrange("p k d c -> p (k d) c"), AX.X, ALU.add)
            link(V.tensor_reduce(coef[:, :], pc.rearrange("p k c d -> p (k c) d"), AX.X, ALU.add))
            dve.wait_ge(roots_ready, 1)
            link(V.reciprocal(nrm[:, 8:12], nrm[:, 4:8]))
            link(V.tensor_tensor(nrm[:, 8:12], nrm[:, 8:12], nrm[:, 0:4], ALU.mult))
            link(V.tensor_tensor(nrm[:, 8:12], nrm[:, 8:12], nrm[:, 4:8], ALU.add))
            link(V.tensor_scalar(nrm[:, 8:12], nrm[:, 8:12], 0.5, None, ALU.mult))
            link(V.reciprocal(nrm[:, 12:16], nrm[:, 8:12]))
            i3 = nrm[:, 12:16].rearrange("p (k s) -> p k s", k=KH)
            link(V.tensor_tensor(nrm[:, 0:2], i3[:, :, 0], i3[:, :, 1], ALU.mult))
            link(V.tensor_tensor(nrm[:, 0:2], nrm[:, 0:2], q3[:, :, 12], ALU.mult))
            for cf, mat, ready in ((coef_t, rot_t, rot_t_ready), (coef, rot, rot_ready)):
                c3 = cf[:, :].rearrange("p (k c) -> p k c", k=KH)
                link(V.tensor_tensor(c3, c3, nrm[:, 0:2].unsqueeze(2).to_broadcast([P, KH, QC]), ALU.mult))
                for k in range(KH):
                    V.tensor_tensor(mat[:, k * P:(k + 1) * P].rearrange("p (c j) -> p c j", c=QC),
                                    mask_j[:, :].unsqueeze(1).to_broadcast([P, QC, JH]),
                                    c3[:, k].unsqueeze(2).to_broadcast([P, QC, JH]), ALU.mult).then_inc(ready, 1)
            dve.wait_ge(wr_turned, 1)
            V.tensor_copy(wr_rot[:, :], late_ps[:, 256:256 + KH * NE]).then_inc(wr_ready, 1)

            ne = "p (n e) -> p n e"
            lg3 = lg[:, :].rearrange(ne, n=NB)
            eq3 = eq[:, :].rearrange(ne, n=NB)
            rev3 = rev[:, :].unsqueeze(1).to_broadcast([P, NB, NE])
            dve.wait_ge(small_loaded, 48)
            dve.wait_ge(logits_ready, 1)
            dve.sem_inc(pair_free, RING)
            link(V.tensor_tensor(lg3, late_ps[:, 0:NB * NE].rearrange(ne, n=NB),
                                 rb[:, :].unsqueeze(1).to_broadcast([P, NB, NE]), ALU.add))
            link(V.tensor_reduce(mx[:, :], lg3, AX.X, ALU.max))
            link(V.tensor_tensor(eq3, lg3, mx[:, :].unsqueeze(2).to_broadcast([P, NB, NE]), ALU.is_ge))
            link(V.tensor_tensor(eq3, eq3, rev3, ALU.mult))
            link(V.tensor_reduce(mx[:, :], eq3, AX.X, ALU.max))
            V.tensor_tensor(oh[:, :].rearrange("p (e n) -> p n e", n=NB), rev3,
                            mx[:, :].unsqueeze(2).to_broadcast([P, NB, NE]), ALU.is_equal).then_inc(oh_ready, 1)

            prefix = xk_ps[1][:, 0:P]
            totals = xk_ps[1][:, P:2 * P]
            gex3 = gex[:, :].rearrange("p (e n) -> p e n", n=NB)
            gin3 = gin[:, :].rearrange("p (e n) -> p e n", n=NB)
            cnt, til, tend, tst, off, zed = (sm[:, a * NE:(a + 1) * NE] for a in range(6))
            dve.wait_ge(ranks_ready, 1)
            link(V.tensor_tensor_scan(gin[:, :], ones[:, :], totals, 0.0, ALU.mult, ALU.add))
            link(V.tensor_tensor(gex[:, :], gin[:, :], totals, ALU.subtract))
            link(V.tensor_tensor(cnt, gin3[:, :, NB - 1], gex3[:, :, 0], ALU.subtract))
            over = ct[:, 0:NE * (TOK // ITEM - 1)].rearrange("p (e m) -> p e m", e=NE)
            link(V.scalar_tensor_tensor(over, cnt.unsqueeze(2).to_broadcast([P, NE, TOK // ITEM - 1]), 1.0 / ITEM,
                                        iota[:, 1:TOK // ITEM].unsqueeze(1).to_broadcast([P, NE, TOK // ITEM - 1]),
                                        ALU.mult, ALU.is_gt))
            link(V.tensor_reduce(til, over, AX.X, ALU.add))
            link(V.tensor_scalar(til, til, 1.0, None, ALU.add))
            link(V.tensor_tensor_scan(tend, ones[:, 0:NE], til, 0.0, ALU.mult, ALU.add))
            link(V.tensor_tensor(tst, tend, til, ALU.subtract))
            link(V.scalar_tensor_tensor(off, tst, float(ITEM), gex3[:, :, 0], ALU.mult, ALU.subtract))
            link(V.tensor_tensor(gex3, gex3, off.unsqueeze(2).to_broadcast([P, NE, NB]), ALU.add))
            link(V.tensor_tensor(pos[:, :], prefix, gex[:, :], ALU.add))
            link(V.tensor_tensor(pos[:, :], pos[:, :], oh[:, :], ALU.mult))
            link(V.tensor_reduce(mx[:, :], pos[:, :].rearrange("p (e n) -> p n e", n=NB), AX.X, ALU.add))
            link(V.tensor_copy(slot[:, :], mx[:, :]))
            V.tensor_single_scalar(slot_q[:, :], slot[:, :], 7, ALU.arith_shift_right)
            link(V.tensor_single_scalar(slot_r[:, :], slot[:, :], P - 1, ALU.bitwise_and))
            link(V.tensor_copy(mx[:, :], slot_r[:, :]))
            TS = TAB * NSUB
            for n in range(NB):
                last = V.tensor_scalar(slot_oh[:, n, :], iota16[:, :], mx[:, n:n + 1], None, ALU.is_equal)
            last.then_inc(slots_ready, 1)
            q_oh3 = q_oh[:, :].rearrange("p (n q) -> p n q", n=NB)
            q_val4 = q_val[:, :].rearrange("p (n s q) -> p n s q", n=NB, s=2)
            link(V.tensor_tensor(q_oh3, iota[:, 0:TS].unsqueeze(1).to_broadcast([P, NB, TS]),
                                 slot_q[:, :].unsqueeze(2).to_broadcast([P, NB, TS]), ALU.is_equal))
            V.tensor_scalar(q_val4[:, :, 0, :], q_oh3, pcol[:, :], None, ALU.mult).then_inc(slots_ready, 1)
            V.tensor_tensor(q_val4[:, :, 1, :], q_oh3, iota[:, 0:NB].unsqueeze(2).to_broadcast([P, NB, TS]),
                            ALU.mult).then_inc(slots_ready, 1)

            dve.wait_ge(idx_summed, 1)
            link(V.tensor_copy(idx_f[:, 0:2 * TS], early_ps[:, 0:2 * TS]))
            V.tensor_scalar(idx_f[:, 2 * TS:3 * TS], idx_f[:, 0:TS], 0.0, float(BIG), ALU.is_equal, ALU.mult)
            link(V.scalar_tensor_tensor(idx_f[:, 0:TS], idx_f[:, 0:TS], float(NB), idx_f[:, TS:2 * TS],
                                        ALU.mult, ALU.add))
            V.tensor_scalar(g_idx[:, :], idx_f[:, 0:TS], -float(NB), 0.0, ALU.add, ALU.max)
            V.scalar_tensor_tensor(s_idx[:, :], idx_f[:, 0:TS], -float(NB), idx_f[:, 2 * TS:3 * TS],
                                   ALU.add, ALU.add).then_inc(idx_ready, 1)

            dve.wait_ge(w1_first_split, W1U)
            dve.sem_inc(w1_split, W1P)

            def over_items(ap):
                return ap.unsqueeze(1).to_broadcast([P, TAB, NE])

            le_s, le_e, eq_s, tmp = (ct[:, a * TAB * NE:(a + 1) * TAB * NE].rearrange("p (i e) -> p i e", e=NE)
                                     for a in range(4))
            i_bc = iota[:, 0:TAB].unsqueeze(2).to_broadcast([P, TAB, NE])
            rem, steps, first, prep, expert, word, tmp3 = (cv[:, a * TAB:(a + 1) * TAB] for a in range(7))
            V.tensor_tensor(le_s, over_items(tst), i_bc, ALU.is_le)
            V.tensor_tensor(le_e, over_items(tend), i_bc, ALU.is_le)
            V.tensor_tensor(eq_s, over_items(tst), i_bc, ALU.is_equal)
            link(V.scalar_tensor_tensor(zed, tst, float(ITEM), cnt, ALU.mult, ALU.add))
            V.tensor_reduce(first, eq_s, AX.X, ALU.add)
            V.tensor_reduce(prep, eq_s[:, :, 0:NE - 1], AX.X, ALU.add)
            V.tensor_reduce(expert, le_e, AX.X, ALU.add)
            link(V.tensor_tensor(tmp, le_s, le_e, ALU.subtract))
            link(V.tensor_tensor(tmp, tmp, over_items(zed), ALU.mult))
            link(V.tensor_reduce(rem, tmp, AX.X, ALU.add))
            link(V.scalar_tensor_tensor(rem, rem, 1.0 / STEP, m4i[:, :], ALU.mult, ALU.add))
            MORE = NSTEP - MIN_STEPS
            tmp_s = ct[:, 0:TAB * MORE].rearrange("p (i m) -> p i m", m=MORE)
            link(V.tensor_tensor(tmp_s, rem.unsqueeze(2).to_broadcast([P, TAB, MORE]),
                                 iota[:, MIN_STEPS:NSTEP].unsqueeze(1).to_broadcast([P, TAB, MORE]), ALU.is_gt))
            V.tensor_reduce(steps, tmp_s, AX.X, ALU.add)
            link(V.tensor_scalar(expert, expert, float(NE - 1), 32.0, ALU.min, ALU.mult))
            link(V.scalar_tensor_tensor(word, first, 16.0, expert, ALU.mult, ALU.add))
            link(V.scalar_tensor_tensor(word, prep, 8.0, word, ALU.mult, ALU.add))
            V.tensor_scalar(ctrl[:, 0:1], tend[:, NE - 1:NE], -1.0, None, ALU.add)
            V.tensor_tensor(ctrl[:, 1:1 + TAB], word, steps, ALU.add).then_inc(ctrl_ready, 1)

            def copy_xt(i, k):
                dve.wait_ge(xg_turned, i * KH + (k + 1))
                V.tensor_copy(xg_t[:, k * ITEM:(k + 1) * ITEM], xk_ps[k][:, :]).then_inc(xg_t_done, 1)

            def split_x(i):
                for k in range(KH):
                    part_k = slice(k * ITEM, (k + 1) * ITEM)
                    dve.wait_ge(xr_hi_done, i * KH + (k + 1))
                    V.tensor_tensor(xr_lo[:, part_k], xk_ps[k][:, :], xr_hi[:, part_k].bitcast(F32), ALU.subtract)\
                        .then_inc(xr_lo_done, 1)

            dve.wait_ge(ctrl_ready, 1)
            last_item = load_last(dve)
            for k in range(KH):
                copy_xt(0, k)
            split_x(0)

            def gated(i, c, n):
                dve.wait_ge(sig_done, i * NC + (c + 1))
                V.scalar_tensor_tensor(u32[:, c % U_RING, 0:n], pair[c % RING][0][:, 0:n], b1_cur[:, c:c + 1],
                                       sig[:, c % RING, 0:n], ALU.add, ALU.mult).then_inc(pair_free, 1)

            def lo_u(i, c, n):
                dve.wait_ge(u_hi_done, i * NC + (c + 1))
                at = (c % U_RING) * ITEM
                V.tensor_tensor(u_lo[:, at:at + n], u32[:, c % U_RING, 0:n], u_hi[:, at:at + n].bitcast(F32),
                                ALU.subtract).then_inc(u_lo_done, 1)

            def lo_part(parity, at, n_hi):
                dve.wait_ge(w1_hi_done, n_hi)
                V.tensor_tensor(w_lo[:, bass.ds(w_col(parity, 0) + at, PIECE)], w_raw[:, at:at + PIECE],
                                w_hi[:, bass.ds(w_col(parity, 0) + at, PIECE)].bitcast(F32), ALU.subtract)\
                    .then_inc(w1_split, 1)

            def add_rows(i, blocks):
                dve.wait_ge(mm2_done, i + 1)
                dve.wait_ge(xb_done, i + 2)
                for h in range(2):
                    n = min(blocks - 2 * h, 2) * DIM
                    V.tensor_tensor(y_out[:, h * 2 * DIM:h * 2 * DIM + n], y_ps[h][:, 0:n],
                                    xb[:, bass.ds((i & 1) * (NSUB * DIM) + h * 2 * DIM, n)],
                                    ALU.add).then_inc(y_done, 1)
                    if blocks <= 2:
                        dve.sem_inc(y_done, 1)
                        break

            def item(i, word, blocks, prep):
                n = blocks * P
                e = f_expert(word)
                dve.wait_ge(b1_cur_done, e + 1)
                for c in range(NC):
                    gated(i, c, n)
                    if c > 0:
                        lo_u(i, c - 1, n)
                    if c in (TURN, TURN + 1):
                        copy_xt(i + 1, c - TURN)
                    if prep:
                        lo_part((e + 1) & 1, c * PIECE, e * W1P + (W1P + c + 1))
                lo_u(i, NC - 1, n)
                split_x(i + 1)
                add_rows(i, blocks)

            dve.wait_ge(b1_t_done, 1)
            with dve.Fori(0, MAX_ITEMS) as i:
                with dve.If(i <= last_item):
                    word = load_word(dve, i)
                    blocks = f_blocks(word)
                    with dve.If(f_first(word) > 0):
                        e = f_expert(word)
                        V.tensor_copy(b1_cur[:, :], b1_t[:, bass.ds(e * (2 * NC), 2 * NC)]).then_inc(b1_cur_done, 1)
                    with dve.If(f_prep(word) > 0):
                        with dve.If(blocks < 1):
                            item(i, word, 2, True)
                        with dve.Else():
                            with dve.If(blocks < 2):
                                item(i, word, 3, True)
                            with dve.Else():
                                item(i, word, 4, True)
                    with dve.Else():
                        with dve.If(blocks < 1):
                            item(i, word, 2, False)
                        with dve.Else():
                            with dve.If(blocks < 2):
                                item(i, word, 3, False)
                            with dve.Else():
                                item(i, word, 4, False)

        @block.tensor
        def _(pe):
            T = nc.tensor
            pe.wait_ge(consts_ready, 6)
            pe.wait_ge(q_repeated, KH)
            for k in range(KH):
                last = T.matmul(late_ps[:, k * 16:(k + 1) * 16], q_rep[:, k * P:(k + 1) * P], ident[0:13, 0:16],
                                start=True, stop=True)
            last.then_inc(q_spread, 1)

            pe.wait_ge(small_loaded, 48)
            T.transpose(early_ps[:, 0:P], b1_rows[:, :], ident[:, :]).then_inc(b1_turned, 1)
            for f in range(NB // 2):
                if f >= 4:
                    pe.wait_ge(x_t_done, f - 3)
                pe.wait_ge(x_loaded[f // 2], 16)
                for a in range(4):
                    xk = x_tok[:, 4 * (f // 2) + a, :].rearrange("p (m k) -> p k m", k=KH)
                    last = T.transpose(turn_ps[f % 4][:, a * P:(a + 1) * P], xk[:, f % 2], ident[:, :])
                last.then_inc(x_turned, 1)
            pe.wait_ge(rot_t_ready, KH)
            for k in range(KH):
                last = T.matmul(late_ps[:, 256 + k * NE:256 + (k + 1) * NE], rot_t[:, k * P:(k + 1) * P],
                                wr[:, k * NE:(k + 1) * NE], start=True, stop=True)
            last.then_inc(wr_turned, 1)
            pe.wait_ge(wr_ready, 1)
            for g in range(4):
                pe.wait_ge(x_t_done, 2 * g + 2)
                if g >= 2:
                    pe.wait_ge(logits_t_done, g - 1)
                for k in range(KH):
                    last = T.matmul(xk_ps[g % 2][0:NE, :], wr_rot[:, k * NE:(k + 1) * NE],
                                    x_t[:, k, g * 512:(g + 1) * 512], start=(k == 0), stop=(k == KH - 1))
                last.then_inc(logits_t_ready, 1)
            for n in range(NB):
                if n % 4 == 0:
                    pe.wait_ge(logits_t_done, n // 4 + 1)
                last = T.transpose(late_ps[:, n * NE:(n + 1) * NE], logits_t[:, n * P:(n + 1) * P], ident[0:NE, 0:NE])
            last.then_inc(logits_ready, 1)
            pe.wait_ge(oh_ready, 1)
            pe.wait_ge(logits_t_done, 4)
            T.matmul(xk_ps[1][:, 0:P], lower[:, :], oh[:, :], start=True, stop=True)
            T.matmul(xk_ps[1][:, P:2 * P], ones16[:, :], oh[:, :], start=True, stop=True).then_inc(ranks_ready, 1)
            TS = TAB * NSUB
            pe.wait_ge(slots_ready, 3)
            pe.wait_ge(b1_t_done, 1)
            for n in range(NB):
                last = T.matmul(early_ps[:, 0:2 * TS], slot_oh[:, n, :], q_val[:, n * 2 * TS:(n + 1) * 2 * TS],
                                start=(n == 0), stop=(n == NB - 1))
            last.then_inc(idx_summed, 1)

            def turn_item(i, k):
                pe.wait_ge(gathered, i * (16 * NSUB) + 16 * NSUB)
                for s in range(NSUB):
                    xk = xg[:, s * DIM:(s + 1) * DIM].rearrange("p (m k) -> p k m", k=KH)
                    last = T.transpose(xk_ps[k][:, s * P:(s + 1) * P], xk[:, k], ident[:, :])
                last.then_inc(xg_turned, 1)

            def rotate(i):
                for k in range(KH):
                    pe.wait_ge(xg_t_done, i * KH + (k + 1))
                    T.matmul(xk_ps[k][:, :], rot[:, k * P:(k + 1) * P], xg_t[:, k * ITEM:(k + 1) * ITEM],
                             start=True, stop=True).then_inc(rotated, 1)

            pe.wait_ge(rot_ready, KH)
            pe.wait_ge(idx_ready, 1)
            for k in range(KH):
                turn_item(0, k)
            rotate(0)
            pe.wait_ge(ctrl_ready, 1)
            last_item = load_last(pe)

            def first_product(i, e, parity, steps, c):
                n = steps * STEP
                if c % 2 == 0:
                    pe.wait_ge(w1_split, e * W1P + (c + 2))
                pe.wait_ge(pair_free, i * NC + (c + 1))
                for ag in range(2):
                    dst = pair[c % RING][ag][:, 0:n]
                    for k in range(KH):
                        if c == 0 and ag == 0:
                            pe.wait_ge(xr_lo_done, i * KH + (k + 1))
                        at = w_col(parity, c // 2) + k * 512 + ag * 256 + (c % 2) * P
                        xh = xr_hi[:, k * ITEM:k * ITEM + n]
                        xl = xr_lo[:, k * ITEM:k * ITEM + n]
                        T.matmul(dst, w_hi[:, at:at + P], xh, start=(k == 0), stop=False)
                        T.matmul(dst, w_hi[:, at:at + P], xl, start=False, stop=False)
                        last = T.matmul(dst, w_lo[:, at:at + P], xh, start=False, stop=(k == KH - 1))
                last.then_inc(mm1_done, 1)

            def second_product(i, e, parity, blocks, c):
                if c % CPU2 == 0:
                    pe.wait_ge(w2_split, e * W2U + (c // CPU2 + 1))
                pe.wait_ge(u_lo_done, i * NC + (c + 1))
                at = w_col(parity, W1U + c // CPU2) + (c % CPU2) * DIM
                wv = slice(at, at + DIM)
                if c == 0:
                    for h in range(blocks // 2):
                        T.matmul(y_ps[h][:, :], ones16[0:1, :], zeros16[:, :], start=True, stop=False)
                for s in range(blocks):
                    uv = slice((c % U_RING) * ITEM + s * P, (c % U_RING) * ITEM + (s + 1) * P)
                    dst = y_ps[s // 2][:, (s % 2) * DIM:(s % 2 + 1) * DIM]
                    T.matmul(dst, u_hi[:, uv], w_hi[:, wv], start=(c == 0 and s // 2 == blocks // 2), stop=False)
                    T.matmul(dst, u_hi[:, uv], w_lo[:, wv], start=False, stop=False)
                    last = T.matmul(dst, u_lo[:, uv], w_hi[:, wv], start=False,
                                    stop=(c == NC - 1 and (s % 2 == 1 or s == blocks - 1)))
                if c == NC - 1:
                    last.then_inc(mm2_done, 1)

            def item(i, word, parity, steps):
                e = f_expert(word)
                blocks = (steps * STEP + P - 1) // P
                for c in range(NC):
                    first_product(i, e, parity, steps, c)
                    if c in (TURN, TURN + 1):
                        turn_item(i + 1, c - TURN)
                    if c == NC - 2:
                        rotate(i + 1)
                    if c >= LAG:
                        second_product(i, e, parity, blocks, c - LAG)
                for c in range(NC - LAG, NC):
                    second_product(i, e, parity, blocks, c)

            def item_of_any_size(i, word, parity):
                more = f_steps(word)
                with pe.If(more < 2):
                    with pe.If(more < 1):
                        item(i, word, parity, MIN_STEPS)
                    with pe.Else():
                        item(i, word, parity, MIN_STEPS + 1)
                with pe.Else():
                    with pe.If(more < 3):
                        item(i, word, parity, MIN_STEPS + 2)
                    with pe.Else():
                        with pe.If(more < 4):
                            item(i, word, parity, MIN_STEPS + 3)
                        with pe.Else():
                            item(i, word, parity, MIN_STEPS + 4)

            with pe.Fori(0, MAX_ITEMS) as i:
                with pe.If(i <= last_item):
                    word = load_word(pe, i)
                    with pe.If((f_expert(word) & 1) < 1):
                        item_of_any_size(i, word, 0)
                    with pe.Else():
                        item_of_any_size(i, word, 1)


_INS = ['x', 'cond_256', 'L0_cond_q_right', 'L0_cond_spectral_gate', 'L0_ffn_router_w', 'L0_ffn_router_b',
        'L0_ffn_w1', 'L0_ffn_b1', 'L0_ffn_w2', 'L0_ffn_b2']
_OUTS = [((8, 256, 256), 'float32')]


def kernel(**inputs):
    import numpy as _np
    import concourse.bacc as _bacc
    from concourse import mybir as _mybir
    from concourse.bass_utils import run_bass_kernel_spmd as _run

    nc = _bacc.Bacc("TRN2", target_bir_lowering=False, num_devices=1)
    arrays, args = {}, []
    for name in _INS:
        a = _np.ascontiguousarray(inputs[name])
        arrays[f"in_{name}_dram"] = a
        args.append(nc.dram_tensor(f"in_{name}_dram", a.shape, _mybir.dt.from_np(a.dtype), kind="ExternalInput").ap())
    for i, (shape, dtype) in enumerate(_OUTS):
        dt = _mybir.dt.from_np(_np.dtype(dtype))
        args.append(nc.dram_tensor(f"out_{i}_dram", shape, dt, kind="ExternalOutput").ap())
    adaln_moe_ffn_kernel(nc, *args)
    r = _run(nc, [arrays], core_ids=[0])
    got = tuple(r.results[0][f"out_{i}_dram"] for i in range(len(_OUTS)))
    return got[0]
```

```python
import concourse.bass as bass
from concourse import mybir
from contextlib import ExitStack


def adaln_moe_ffn_kernel(nc, x, cond, q_right, gate, router_w, router_b, w1, b1, w2, b2, out):
    F32 = mybir.dt.float32
    F32R = mybir.dt.float32r
    BF16 = mybir.dt.bfloat16
    F16 = mybir.dt.float16
    I32 = mybir.dt.int32
    ALU = mybir.AluOpType
    ACT = mybir.ActivationFunctionType
    AX = mybir.AxisListType

    P = 128
    BATCH, SEQ, DIM = x.shape
    TOK = BATCH * SEQ
    NB = TOK // P
    NE = router_w.shape[1]
    HID = w2.shape[1]
    QC = 4
    QD = DIM // QC
    KH = DIM // P
    JH = QD // KH
    NC = HID // P
    ITEM = 512
    NSUB = ITEM // P
    SIZES = (256, 288, 320, 352, 384, 448, 512)
    BLOCKS = [(size + P - 1) // P for size in SIZES]
    MAX_ITEMS = TOK // ITEM + NE - 1
    TAB = MAX_ITEMS + 2
    UNIT = 1024
    W1U = KH * 2 * HID // UNIT
    W2U = HID // P * DIM // UNIT
    WU = W1U + W2U
    CPU2 = UNIT // DIM
    PIECE = UNIT // 2
    W1P = W1U * UNIT // PIECE
    W2P = W2U * UNIT // PIECE
    RING = 2
    U_RING = 5
    LAG = 3
    PREP = ((0,), (1,), (2,), (3, 8), (4, 9), (5, 10), (6,), ())
    PREP_LAST = (7, 11)
    BIG = 4096
    EPS = 1e-8

    x_flat = x.rearrange("b s d -> (b s) d")
    out_flat = out.rearrange("b s d -> (b s) d")
    x_pair = nc.dram_tensor("x_pair", (TOK, 2 * DIM), F32, kind="Internal").ap()

    ctx = ExitStack()
    with ctx:
        def sb(name, cols, dt=F32, rows=P):
            return ctx.enter_context(nc.sbuf_tensor(name, [rows, cols], dt))

        def ps(name):
            return ctx.enter_context(nc.psum_tensor(name, [P, 512], F32))

        def sem(name):
            return ctx.enter_context(nc.semaphore(name))

        w_raw = sb("w_raw", WU * UNIT)
        w_hi = sb("w_hi", 2 * WU * UNIT, F32R)
        w_lo = sb("w_lo", 2 * WU * UNIT, F32R)
        arena = sb("arena", NB * DIM)
        x_tok = arena[:, :].rearrange("p (n d) -> p n d", n=NB)
        x_rot = x_tok
        u32 = arena[:, 0:U_RING * ITEM].rearrange("p (c t) -> p c t", c=U_RING)
        sig = arena[:, U_RING * ITEM:(U_RING + RING) * ITEM].rearrange("p (c t) -> p c t", c=RING)
        arena_t = sb("arena_t", NB * DIM)
        x_t = arena_t[:, :].rearrange("p (k t) -> p k t", k=KH)
        xb = arena_t[:, 0:2 * NSUB * DIM]
        u_hi = sb("u_hi", U_RING * ITEM, F32R)
        u_lo = sb("u_lo", U_RING * ITEM, F32R)
        xr_hi = sb("xr_hi", KH * ITEM, F32R)
        xr_lo = sb("xr_lo", KH * ITEM, F32R)
        xg = sb("xg", NSUB * 2 * DIM)
        logits_t = xg[0:NE, 0:TOK]
        y_out = sb("y_out", NSUB * DIM)
        b1_t = sb("b1_t", P)
        b2_all = sb("b2_all", NE * DIM)
        g_cur = sb("g_cur", NSUB, I32)
        s_cur = sb("s_cur", NSUB, I32)
        g_idx = sb("g_idx", TAB * NSUB, I32)
        s_idx = sb("s_idx", TAB * NSUB, I32)
        ctrl = sb("ctrl", 1 + TAB, I32)
        ident = sb("ident", P)
        iota = sb("iota", P)
        lower = sb("lower", P, BF16)
        ones16 = sb("ones16", P, BF16)
        ones = sb("ones", P)
        zeros16 = sb("zeros16", 2 * DIM, BF16, rows=1)
        tok_1 = sb("tok_1", NB)
        sizes = sb("sizes", len(SIZES) - 1)
        table_warm = sb("table_warm", 1)
        rev = sb("rev", NE)
        before = sb("before", TAB)
        mask_j = sb("mask_j", JH)
        mask_c = sb("mask_c", QC)
        taken = [0]

        def early(rows, cols):
            taken[0] += cols
            return b2_all[0:rows, taken[0] - cols:taken[0]]

        q_rows = sb("q_rows", QD, rows=13)
        b1_rows = early(P, P)
        sgn_l = early(P, 64)
        sgn_r = early(P, 64)
        q_rep = early(13, KH * P)
        qv = sb("qv", KH * 16)
        qsq = sb("qsq", KH * 16)
        nrm = sb("nrm", 4 * KH * 2)
        mats = sb("mats", 2 * KH * 16)
        prod = early(P, KH * 64)
        r_full = sb("r_full", KH * 16)
        coef = sb("coef", KH * QC)
        coef_t = sb("coef_t", KH * QC)
        rot = early(P, KH * P)
        rot_t = early(P, KH * P)
        iota16 = sb("iota16", P, BF16)
        wr = sb("wr", KH * NE)
        wr_rot = sb("wr_rot", KH * NE)
        rb = sb("rb", NE)
        mx = sb("mx", NB)
        oh = sb("oh", NB * NE, BF16)
        sm = sb("sm", 8 * NE)
        slot = sb("slot", NB, I32)
        slot_q = sb("slot_q", NB, I32)
        slot_r = sb("slot_r", NB, I32)
        q16 = sb("q16", NB, BF16)
        r16 = sb("r16", NB, BF16)
        idx_f = sb("idx_f", 2 * TAB * NSUB)

        def part(a, at, cols):
            return a[:, at:at + cols]

        ct = part(y_out, 0, 4 * TAB * NE)
        cv = part(y_out, 4 * TAB * NE, 8 * TAB)
        lg, eq, gin, gex, pos = (part(xg, a * NB * NE, NB * NE) for a in range(5))
        slot_oh = part(xg, 5 * NB * NE, NB * P // 2).bitcast(F16).rearrange("p (n r) -> p n r", n=NB)
        q_val = part(y_out, 4 * TAB * NE + 8 * TAB, NB * TAB * NSUB // 2).bitcast(F16)

        pair = [[ps(f"{ag}{b}_ps") for ag in "ag"] for b in range(RING)]
        y_ps = [ps(f"y{h}_ps") for h in range(2)]
        xk_ps = [ps(f"xk{k}_ps") for k in range(KH)]
        turn_ps = pair[0] + pair[1]
        early_ps, late_ps = y_ps

        consts_ready = sem("consts_ready")
        pool_chain = sem("pool_chain")
        dve_chain = sem("dve_chain")
        q_loaded = sem("q_loaded")
        small_loaded = sem("small_loaded")
        b2_loaded = sem("b2_loaded")
        x_loaded = [sem(f"x_loaded{g}") for g in range(4)]
        w_loaded = [sem(f"w_loaded{u}") for u in range(WU)]
        q_repeated = sem("q_repeated")
        q_spread = sem("q_spread")
        sums_ready = sem("sums_ready")
        roots_ready = sem("roots_ready")
        rot_ready = sem("rot_ready")
        rot_t_ready = sem("rot_t_ready")
        wr_turned = sem("wr_turned")
        wr_ready = sem("wr_ready")
        b1_turned = sem("b1_turned")
        b1_t_done = sem("b1_t_done")
        x_turned = sem("x_turned")
        x_t_done = sem("x_t_done")
        logits_t_ready = sem("logits_t_ready")
        logits_t_done = sem("logits_t_done")
        logits_ready = sem("logits_ready")
        oh_ready = sem("oh_ready")
        ranks_ready = sem("ranks_ready")
        q_oh_ready = sem("q_oh_ready")
        q_val_ready = sem("q_val_ready")
        slots_ready = sem("slots_ready")
        idx_summed = sem("idx_summed")
        ctrl_ready = sem("ctrl_ready")
        idx_ready = sem("idx_ready")
        w1_hi_done = sem("w1_hi_done")
        w2_hi_done = sem("w2_hi_done")
        w1_first_split = sem("w1_first_split")
        w1_split = sem("w1_split")
        w2_split = sem("w2_split")
        gathered = [sem(f"gathered{s}") for s in range(NSUB)]
        scattered = [sem(f"scattered{h}") for h in range(2)]
        g_cur_set = sem("g_cur_set")
        s_cur_set = sem("s_cur_set")
        xb_done = sem("xb_done")
        xg_turned = sem("xg_turned")
        rot_x_ready = sem("rot_x_ready")
        x_rot_done = sem("x_rot_done")
        x_pair_written = sem("x_pair_written")
        xr_hi_done = sem("xr_hi_done")
        xr_lo_done = sem("xr_lo_done")
        g_done = sem("g_done")
        a_done = sem("a_done")
        sig_done = sem("sig_done")
        pair_free = sem("pair_free")
        u_hi_done = sem("u_hi_done")
        u_lo_done = sem("u_lo_done")
        mm2_done = sem("mm2_done")
        y_done = sem("y_done")

        block = ctx.enter_context(nc.Block())

        TS = TAB * NSUB
        q_val3 = q_val[:, :].rearrange("p (n q) -> p n q", n=NB)

        def w_col(parity, unit):
            return parity * (WU * UNIT) + unit * UNIT

        def f_size(w):
            return w & 7

        def if_blocks(eng, word, body):
            with eng.If(f_size(word) < BLOCKS.index(3)):
                body(2)
            with eng.Else():
                with eng.If(f_size(word) < BLOCKS.index(4)):
                    body(3)
                with eng.Else():
                    body(4)

        def f_prep(w):
            return (w >> 3) & 1

        def f_expert(w):
            return (w >> 4) & (NE - 1)

        def load_last(eng):
            return eng.value_load(ctrl[0:1, 0:1], min_val=NE - 1, max_val=MAX_ITEMS - 1)

        def load_word(eng, i):
            return eng.value_load(ctrl[0:1, bass.ds(i + 1, 1)], min_val=0, max_val=127)

        def first_word(eng):
            next_word = eng.alloc_register("next_word")
            eng.reg_load(next_word, ctrl[0:1, 1:2])
            return next_word

        def this_word(eng, next_word):
            return eng.snap(next_word, min_val=0, max_val=127)

        def load_next_word(eng, next_word, i):
            eng.reg_load(next_word, ctrl[0:1, bass.ds(i + 2, 1)])

        @block.sync
        def _(sp):
            sp.dma_start(q_rows[0:8, :], cond).then_inc(q_loaded, 16)
            sp.dma_start(q_rows[12:13, :], gate.rearrange("a b c j -> (a b c) j")).then_inc(q_loaded, 16)
            xv = x_flat.rearrange("(p n) d -> p n d", p=P)
            for g in range(4):
                sp.dma_start(x_tok[:, 4 * g:4 * g + 4, :], xv[:, 4 * g:4 * g + 4, :]).then_inc(x_loaded[g], 16)

            w1_v = w1.rearrange("e (m k) (ag f) -> e m (k ag) f", k=KH, ag=2)
            w2_v = w2.rearrange("e (h c p) d -> e h p c d", h=W2U, p=P)

            def load_unit(e, u):
                if u < W1U:
                    dst = w_raw[:, u * UNIT:(u + 1) * UNIT].rearrange("p (b f) -> p b f", b=2 * KH)
                    sp.dma_start(dst, w1_v[e, :, :, u * 256:(u + 1) * 256]).then_inc(w_loaded[u], 16)
                else:
                    dst = w_raw[:, u * UNIT:(u + 1) * UNIT].rearrange("p (c d) -> p c d", d=DIM)
                    sp.dma_start(dst, w2_v[e, u - W1U]).then_inc(w_loaded[u], 16)

            for u in range(WU):
                load_unit(0, u)
            sp.dma_start(x_pair[:, 0:DIM], x_flat).then_inc(x_pair_written, 16)
            for s in range(NSUB):
                sp.wait_ge(gathered[s], 16)
            sp.dma_start(b2_all[:, :], b2.rearrange("e d -> (e d)").partition_broadcast(P)).then_inc(b2_loaded, 16)
            for u in range(WU):
                if u < W1U:
                    sp.wait_ge(w1_first_split, u + 1)
                else:
                    sp.wait_ge(w2_split, u - W1U + 1)
                load_unit(1, u)
            with sp.Fori(2, NE) as e:
                for u in range(WU):
                    if u < W1U:
                        sp.wait_ge(w1_split, e * W1P - (W1P - 2 * u - 2))
                    else:
                        sp.wait_ge(w2_split, e * W2U - (W2U - (u - W1U) - 1))
                    load_unit(e, u)

        @block.gpsimd
        def _(pool):
            count = [0]

            def link(ins):
                count[0] += 1
                ins.then_inc(pool_chain, 1)
                pool.wait_ge(pool_chain, count[0])

            nc.gpsimd.memset(ones[:, :], 1.0).then_inc(pool_chain, 1)
            nc.gpsimd.memset(ones16[:, :], 1.0).then_inc(pool_chain, 1)
            nc.gpsimd.memset(sgn_l[:, :], 0.0).then_inc(pool_chain, 1)
            nc.gpsimd.memset(sgn_r[:, :], 0.0).then_inc(pool_chain, 1)
            count[0] = 4
            pool.wait_ge(pool_chain, count[0])
            nc.gpsimd.affine_select(out=ident[:, :], in_=ones[:, :], compare_op=ALU.is_equal, fill=0.0,
                                    base=0, pattern=[[-1, P]], channel_multiplier=1).then_inc(consts_ready, 1)
            left = ((1, -1, -1, -1), (1, 1, -1, 1), (1, 1, 1, -1), (1, -1, 1, 1))
            right = ((1, -1, -1, -1), (1, 1, 1, -1), (1, -1, 1, 1), (1, 1, -1, 1))
            for a in range(QC):
                for b in range(QC):
                    m = a ^ b
                    conj = 1 if m == 0 else -1
                    nc.gpsimd.memset(sgn_l[:, a * 16 + b * 4 + m:a * 16 + b * 4 + m + 1], float(left[a][b]))
                    last = nc.gpsimd.memset(sgn_r[:, a * 16 + b * 4 + m:a * 16 + b * 4 + m + 1],
                                            float(right[a][b] * conj))
            last.then_inc(consts_ready, 1)
            nc.gpsimd.iota(iota[:, :], pattern=[[1, P]], base=0, channel_multiplier=0,
                           allow_small_or_imprecise_dtypes=True).then_inc(consts_ready, 1)
            nc.gpsimd.iota(iota16[:, :], pattern=[[1, P]], base=0, channel_multiplier=0,
                           allow_small_or_imprecise_dtypes=True).then_inc(consts_ready, 1)
            nc.gpsimd.iota(tok_1[:, :], pattern=[[1, NB]], base=1, channel_multiplier=NB,
                           allow_small_or_imprecise_dtypes=True).then_inc(consts_ready, 1)
            nc.gpsimd.affine_select(out=lower[:, :], in_=ones16[:, :], compare_op=ALU.is_ge, fill=0.0,
                                    base=-1, pattern=[[1, P]], channel_multiplier=-1).then_inc(consts_ready, 1)

            for m, size in enumerate(SIZES[:-1]):
                nc.gpsimd.memset(sizes[:, m:m + 1], float(size))
            nc.gpsimd.memset(y_out[:, :], 0.0).then_inc(consts_ready, 1)
            nc.gpsimd.memset(zeros16[:, :], 0.0).then_inc(consts_ready, 1)

            def lo_unit(parity, u, done, hi_done, n_hi):
                pool.wait_ge(hi_done, n_hi)
                nc.gpsimd.tensor_tensor(w_lo[:, bass.ds(w_col(parity, u), UNIT)],
                                        w_raw[:, u * UNIT:(u + 1) * UNIT],
                                        w_hi[:, bass.ds(w_col(parity, u), UNIT)].bitcast(F32),
                                        ALU.subtract).then_inc(done, 1)

            for u in range(W1U):
                lo_unit(0, u, w1_first_split, w1_hi_done, 2 * u + 2)
            lo_unit(0, W1U, w2_split, w2_hi_done, 2)

            pool.wait_ge(q_oh_ready, 1)
            nc.gpsimd.tensor_tensor(q_val3, q_val3, tok_1[:, :].unsqueeze(2).to_broadcast([P, NB, TS]), ALU.mult)\
                .then_inc(q_val_ready, 1)

            row_bound = pool.to_reg(TOK - 1)

            def issue_gather(idx):
                for s in range(NSUB):
                    nc.gpsimd.indirect_dma_start(
                        out=xg[:, s * 2 * DIM:(s + 1) * 2 * DIM], out_offset=None, in_=x_pair,
                        in_offset=bass.IndirectOffsetOnAxis(ap=idx[:, s:s + 1], axis=0),
                        bounds_check=row_bound, oob_is_err=False).then_inc(gathered[s], 16)

            def add_b2(i, word):
                e = f_expert(word)
                dst = xb[:, bass.ds((i & 1) * (NSUB * DIM), NSUB * DIM)]
                nc.gpsimd.tensor_tensor(
                    dst.rearrange("p (s d) -> p s d", s=NSUB),
                    xg[:, :].rearrange("p (s d) -> p s d", s=NSUB)[:, :, 0:DIM],
                    b2_all[:, bass.ds(e * DIM, DIM)].unsqueeze(1).to_broadcast([P, NSUB, DIM]),
                    ALU.add).then_inc(xb_done, 1)

            pool.wait_ge(x_pair_written, 5 * 16)
            pool.wait_ge(idx_ready, 1)
            issue_gather(g_idx[:, 0:NSUB])
            for u in range(1, W2U):
                lo_unit(0, W1U + u, w2_split, w2_hi_done, 2 * u + 2)
            pool.wait_ge(ctrl_ready, 1)
            last_item = load_last(pool)
            pool.wait_ge(b2_loaded, 16)
            for s in range(NSUB):
                pool.wait_ge(gathered[s], 16)
            add_b2(0, load_word(pool, 0))
            pool.wait_ge(xb_done, 1)
            pool.wait_ge(xg_turned, KH)
            issue_gather(g_idx[:, NSUB:2 * NSUB])

            scattered_1 = pool.alloc_register("scattered_1")
            pool.reg_mov(scattered_1, 32)

            def wait_scattered(items):
                signals_0 = pool.to_reg(items * 32)
                signals_1 = pool.to_reg(pool.snap(scattered_1, min_val=32, max_val=32 * MAX_ITEMS) & 1023)
                pool.wait_ge(scattered[0], signals_0)
                pool.wait_ge(scattered[1], signals_1)

            def item(i, first=False):
                word = load_word(pool, i)
                if not first:
                    wait_scattered(i)
                for s in range(NSUB):
                    pool.wait_ge(gathered[s], i * 16 + 32)
                add_b2(i + 1, load_word(pool, i + 1))
                def prepare(u):
                    with pool.If(f_prep(word) > 0):
                        e = f_expert(word)
                        lo_unit((e + 1) & 1, W1U + u, w2_split, w2_hi_done, e * W2P + (W2P + 2 * u + 2))

                def load_ahead():
                    pool.wait_ge(xb_done, i + 2)
                    pool.wait_ge(xg_turned, i * KH + 2 * KH)
                    nc.gpsimd.tensor_copy(g_cur[:, :], g_idx[:, bass.ds(i * NSUB + 2 * NSUB, NSUB)])\
                        .then_inc(g_cur_set, 1)
                    g_cur_at = pool.to_reg(i + 1)
                    pool.wait_ge(idx_ready, 1)
                    pool.wait_ge(g_cur_set, g_cur_at)
                    issue_gather(g_cur)

                prepare(0)
                if first:
                    load_ahead()
                else:
                    with pool.If(i < last_item):
                        load_ahead()

                prepare(1)
                nc.gpsimd.tensor_copy(s_cur[:, :], s_idx[:, bass.ds(i * NSUB, NSUB)]).then_inc(s_cur_set, 1)
                s_cur_at = pool.to_reg(i + 1)

                def scatter(h):
                    y_at = pool.to_reg(i * 2 + (h + 1))
                    pool.wait_ge(idx_ready, 1)
                    pool.wait_ge(s_cur_set, s_cur_at)
                    pool.wait_ge(y_done, y_at)
                    for s in (2 * h, 2 * h + 1):
                        nc.gpsimd.indirect_dma_start(
                            out=out_flat, out_offset=bass.IndirectOffsetOnAxis(ap=s_cur[:, s:s + 1], axis=0),
                            in_=y_out[:, s * DIM:(s + 1) * DIM], in_offset=None,
                            bounds_check=row_bound, oob_is_err=False).then_inc(scattered[h], 16)

                scatter(0)
                if first:
                    scatter(1)
                else:
                    with pool.If(f_size(word) >= BLOCKS.index(3)):
                        scatter(1)
                        pool.reg_add(scattered_1, scattered_1, 32)

            item(0, first=True)
            with pool.Fori(1, MAX_ITEMS) as i:
                with pool.If(i <= last_item):
                    item(i)
            wait_scattered(last_item + 1)
            for s in range(NSUB):
                pool.wait_ge(gathered[s], last_item * 16 + 32)

        @block.scalar
        def _(act):
            act.dma_start(q_rows[8:12, :], q_right).then_inc(q_loaded, 16)
            act.dma_start(wr[:, :], router_w.rearrange("(m k) e -> m (k e)", k=KH)).then_inc(small_loaded, 16)
            act.dma_start(rb[:, :], router_b.partition_broadcast(P)).then_inc(small_loaded, 16)
            act.dma_start(b1_rows[:, :], b1.rearrange("e (c f) -> (e c) f", f=P)).then_inc(small_loaded, 16)

            for f in range(NB // 2):
                if f == 0:
                    act.wait_ge(sums_ready, 1)
                    nc.scalar.activation(nrm[:, 4:8], nrm[:, 0:4], ACT.Sqrt).then_inc(roots_ready, 1)
                act.wait_ge(x_turned, f + 1)
                nc.scalar.activation(x_t[:, f % 2, (f // 2) * 512:(f // 2 + 1) * 512], turn_ps[f % 4][:, :], ACT.Copy)\
                    .then_inc(x_t_done, 1)
            act.wait_ge(b1_turned, 1)
            nc.scalar.activation(b1_t[:, :], early_ps[:, 0:P], ACT.Copy).then_inc(b1_t_done, 1)
            def hi_part(parity, at, cols, n_loaded):
                u = at // UNIT
                act.wait_ge(w_loaded[u], n_loaded)
                nc.scalar.activation(w_hi[:, bass.ds(w_col(parity, 0) + at, cols)], w_raw[:, at:at + cols], ACT.Copy)\
                    .then_inc(w1_hi_done if u < W1U else w2_hi_done, cols // PIECE)

            for g in range(4):
                act.wait_ge(logits_t_ready, g + 1)
                nc.scalar.activation(logits_t[:, g * 512:(g + 1) * 512], xk_ps[g % 2][0:NE, :], ACT.Copy)\
                    .then_inc(logits_t_done, 1)
                hi_part(0, g * UNIT, UNIT, 16)
            x_pair_v = x_pair.rearrange("(p n) d -> p n d", p=P)
            for b in range(NB // 2):
                act.wait_ge(rot_x_ready, b + 1)
                nc.scalar.activation(x_rot[:, 2 * b:2 * b + 2, :], turn_ps[b % 4][:, :].rearrange("p (n d) -> p n d", n=2),
                                     ACT.Copy).then_inc(x_rot_done, 1)
                if b % 2 == 1:
                    act.wait_ge(x_rot_done, b + 1)
                    act.dma_start(x_pair_v[:, 2 * b - 2:2 * b + 2, DIM:2 * DIM], x_rot[:, 2 * b - 2:2 * b + 2, :])\
                        .then_inc(x_pair_written, 16)
                if b < WU - 4:
                    hi_part(0, (4 + b) * UNIT, UNIT, 16)

            def split_x(i):
                for k in range(KH):
                    act.wait_ge(xg_turned, i * KH + (k + 1))
                    nc.scalar.activation(xr_hi[:, k * ITEM:(k + 1) * ITEM], xk_ps[k][:, :], ACT.Copy)\
                        .then_inc(xr_hi_done, 1)

            act.wait_ge(x_rot_done, NB // 2)
            act.sem_inc(sig_done, RING)
            act.wait_ge(ctrl_ready, 1)
            last_item = load_last(act)
            next_word = first_word(act)
            split_x(0)

            def gates(i, e, c, n):
                act.wait_ge(g_done, i * NC + (c + 1))
                nc.scalar.activation(sig[:, c % RING, 0:n], pair[c % RING][1][:, 0:n], ACT.Sigmoid,
                                     bias=b1_t[:, bass.ds(e * (2 * NC) + (NC + c), 1)]).then_inc(sig_done, 1)

            def hi_u(i, c, n):
                act.wait_ge(pair_free, i * NC + (RING + c + 1))
                at = (c % U_RING) * ITEM
                nc.scalar.activation(u_hi[:, at:at + n], u32[:, c % U_RING, 0:n], ACT.Copy).then_inc(u_hi_done, 1)

            def item(i, word, n, prep):
                e = f_expert(word)
                nc.scalar.activation(table_warm[:, :], ones[:, 0:1], ACT.Sigmoid)
                for c in range(NC):
                    gates(i, e, c, n)
                    if prep:
                        for part in PREP[c]:
                            hi_part((e + 1) & 1, part * PIECE, PIECE, e * 16 + 32)
                    if c == NC - 1:
                        load_next_word(act, next_word, i)
                    hi_u(i, c, n)
                split_x(i + 1)
                if prep:
                    for part in PREP_LAST:
                        hi_part((e + 1) & 1, part * PIECE, PIECE, e * 16 + 32)

            with act.Fori(0, MAX_ITEMS) as i:
                with act.If(i <= last_item):
                    word = this_word(act, next_word)
                    with act.If(f_prep(word) > 0):
                        if_blocks(act, word, lambda blocks: item(i, word, blocks * P, True))
                    with act.Else():
                        if_blocks(act, word, lambda blocks: item(i, word, blocks * P, False))

        @block.vector
        def _(dve):
            count = [0]

            def link(ins):
                count[0] += 1
                ins.then_inc(dve_chain, 1)
                dve.wait_ge(dve_chain, count[0])

            V = nc.vector
            dve.wait_ge(q_loaded, 48)
            for k in range(KH):
                V.tensor_copy(q_rep[:, k * P:(k + 1) * P].rearrange("r (c j) -> r c j", c=QC),
                              q_rows[:, :].rearrange("r (j k) -> r k j", k=KH)[:, k].unsqueeze(1)
                              .to_broadcast([13, QC, JH])).then_inc(q_repeated, 1)
            dve.wait_ge(consts_ready, 1)
            V.tensor_reduce(mask_j[:, :], ident[:, :].rearrange("p (c j) -> p j c", c=QC), AX.X, ALU.add)
            V.tensor_reduce(mask_c[:, :], ident[:, :].rearrange("p (c j) -> p c j", c=QC), AX.X, ALU.add)
            dve.wait_ge(q_spread, 1)
            link(V.tensor_copy(qv[:, :], late_ps[:, 0:KH * 16]))
            q3 = qv[:, :].rearrange("p (k r) -> p k r", k=KH)
            s3 = qsq[:, :].rearrange("p (k r) -> p k r", k=KH)
            link(V.tensor_tensor(qsq[:, :], qv[:, :], qv[:, :], ALU.mult))
            n3 = nrm[:, 0:4].rearrange("p (k s) -> p k s", k=KH)
            V.tensor_reduce(n3[:, :, 0], s3[:, :, 0:8], AX.X, ALU.add)
            link(V.tensor_reduce(n3[:, :, 1], s3[:, :, 8:12], AX.X, ALU.add))
            V.tensor_scalar(nrm[:, 0:4], nrm[:, 0:4], EPS, None, ALU.add).then_inc(sums_ready, 1)
            dve.wait_ge(consts_ready, 2)
            ml = mats[:, 0:KH * 16].rearrange("p (k e) -> p k e", k=KH)
            mr = mats[:, KH * 16:2 * KH * 16].rearrange("p (k e) -> p k e", k=KH)
            p4 = prod[:, :].rearrange("p (k e m) -> p k e m", k=KH, m=QC)

            def signed(sgn, r0):
                for k in range(KH):
                    last = V.tensor_tensor(p4[:, k], sgn[:, :].rearrange("p (e m) -> p e m", m=QC),
                                           q3[:, k, r0:r0 + 4].unsqueeze(1).to_broadcast([P, 16, QC]), ALU.mult)
                return last

            link(signed(sgn_l, 0))
            link(V.tensor_reduce(ml, p4, AX.X, ALU.add))
            signed(sgn_r, 8)
            dve.wait_ge(roots_ready, 1)
            link(V.reciprocal(nrm[:, 8:12], nrm[:, 4:8]))
            V.tensor_reduce(mr, p4, AX.X, ALU.add)
            link(V.tensor_tensor(nrm[:, 8:12], nrm[:, 8:12], nrm[:, 0:4], ALU.mult))
            for k in range(KH):
                V.tensor_tensor(
                    prod[:, k * 64:(k + 1) * 64].rearrange("p (c d b) -> p c d b", c=QC, d=QC),
                    ml[:, k].rearrange("p (c b) -> p c b", c=QC).unsqueeze(2).to_broadcast([P, QC, QC, QC]),
                    mr[:, k].rearrange("p (b d) -> p d b", b=QC).unsqueeze(1).to_broadcast([P, QC, QC, QC]),
                    ALU.mult)
            link(V.tensor_tensor(nrm[:, 8:12], nrm[:, 8:12], nrm[:, 4:8], ALU.add))
            V.tensor_reduce(r_full[:, :], prod[:, :].rearrange("p (e b) -> p e b", b=QC), AX.X, ALU.add)
            link(V.tensor_scalar(nrm[:, 8:12], nrm[:, 8:12], 0.5, None, ALU.mult))
            r4 = r_full[:, :].rearrange("p (k c d) -> p k c d", k=KH, c=QC)
            mc = mask_c[:, :].unsqueeze(1).to_broadcast([P, QC, QC])
            pt = prod[:, 0:KH * 16].rearrange("p (k d c) -> p k d c", k=KH, d=QC)
            pc = prod[:, KH * 16:2 * KH * 16].rearrange("p (k c d) -> p k c d", k=KH, c=QC)
            for k in range(KH):
                V.tensor_tensor(pt[:, k], r4[:, k].rearrange("p c d -> p d c"), mc, ALU.mult)
                V.tensor_tensor(pc[:, k], r4[:, k], mc, ALU.mult)
            link(V.reciprocal(nrm[:, 12:16], nrm[:, 8:12]))
            V.tensor_reduce(coef_t[:, :], pt.rearrange("p k d c -> p (k d) c"), AX.X, ALU.add)
            V.tensor_reduce(coef[:, :], pc.rearrange("p k c d -> p (k c) d"), AX.X, ALU.add)
            i3 = nrm[:, 12:16].rearrange("p (k s) -> p k s", k=KH)
            link(V.tensor_tensor(nrm[:, 0:2], i3[:, :, 0], i3[:, :, 1], ALU.mult))
            link(V.tensor_tensor(nrm[:, 0:2], nrm[:, 0:2], q3[:, :, 12], ALU.mult))
            for cf, mat, ready in ((coef_t, rot_t, rot_t_ready), (coef, rot, rot_ready)):
                c3 = cf[:, :].rearrange("p (k c) -> p k c", k=KH)
                link(V.tensor_tensor(c3, c3, nrm[:, 0:2].unsqueeze(2).to_broadcast([P, KH, QC]), ALU.mult))
                for k in range(KH):
                    V.tensor_tensor(mat[:, k * P:(k + 1) * P].rearrange("p (c j) -> p c j", c=QC),
                                    mask_j[:, :].unsqueeze(1).to_broadcast([P, QC, JH]),
                                    c3[:, k].unsqueeze(2).to_broadcast([P, QC, JH]), ALU.mult).then_inc(ready, 1)
            dve.wait_ge(consts_ready, 8)
            dve.wait_ge(wr_turned, 1)
            V.tensor_copy(wr_rot[:, :], late_ps[:, 256:256 + KH * NE]).then_inc(wr_ready, 1)

            V.tensor_scalar(rev[:, :], iota[:, 0:NE], -1.0, float(NE), ALU.mult, ALU.add)
            V.tensor_scalar(before[:, :], iota[:, 0:TAB], -float(ITEM), None, ALU.mult)

            ne = "p (n e) -> p n e"
            lg3 = lg[:, :].rearrange(ne, n=NB)
            eq3 = eq[:, :].rearrange(ne, n=NB)
            rev3 = rev[:, :].unsqueeze(1).to_broadcast([P, NB, NE])
            dve.wait_ge(small_loaded, 48)
            dve.wait_ge(logits_ready, 1)
            link(V.tensor_tensor(lg3, late_ps[:, 0:NB * NE].rearrange(ne, n=NB),
                                 rb[:, :].unsqueeze(1).to_broadcast([P, NB, NE]), ALU.add))
            link(V.tensor_reduce(mx[:, :], lg3, AX.X, ALU.max))
            link(V.tensor_tensor(eq3, lg3, mx[:, :].unsqueeze(2).to_broadcast([P, NB, NE]), ALU.is_ge))
            link(V.tensor_tensor(eq3, eq3, rev3, ALU.mult))
            link(V.tensor_reduce(mx[:, :], eq3, AX.X, ALU.max))
            V.tensor_tensor(oh[:, :].rearrange("p (e n) -> p n e", n=NB), rev3,
                            mx[:, :].unsqueeze(2).to_broadcast([P, NB, NE]), ALU.is_equal).then_inc(oh_ready, 1)

            prefix = xk_ps[1][:, 0:P]
            totals = xk_ps[1][:, P:2 * P]
            gex3 = gex[:, :].rearrange("p (e n) -> p e n", n=NB)
            gin3 = gin[:, :].rearrange("p (e n) -> p e n", n=NB)
            cnt, til, tend, tst, off, zed = (sm[:, a * NE:(a + 1) * NE] for a in range(6))
            dve.wait_ge(ranks_ready, 1)
            link(V.tensor_tensor_scan(gin[:, :], ones[:, :], totals, 0.0, ALU.mult, ALU.add))
            link(V.tensor_tensor(gex[:, :], gin[:, :], totals, ALU.subtract))
            link(V.tensor_tensor(cnt, gin3[:, :, NB - 1], gex3[:, :, 0], ALU.subtract))
            over = ct[:, 0:NE * (TOK // ITEM - 1)].rearrange("p (e m) -> p e m", e=NE)
            link(V.scalar_tensor_tensor(over, cnt.unsqueeze(2).to_broadcast([P, NE, TOK // ITEM - 1]), 1.0 / ITEM,
                                        iota[:, 1:TOK // ITEM].unsqueeze(1).to_broadcast([P, NE, TOK // ITEM - 1]),
                                        ALU.mult, ALU.is_gt))
            link(V.tensor_reduce(til, over, AX.X, ALU.add))
            link(V.tensor_scalar(til, til, 1.0, None, ALU.add))
            link(V.tensor_tensor_scan(tend, ones[:, 0:NE], til, 0.0, ALU.mult, ALU.add))
            link(V.tensor_tensor(tst, tend, til, ALU.subtract))
            link(V.scalar_tensor_tensor(off, tst, float(ITEM), gex3[:, :, 0], ALU.mult, ALU.subtract))
            link(V.tensor_tensor(gex3, gex3, off.unsqueeze(2).to_broadcast([P, NE, NB]), ALU.add))
            link(V.tensor_tensor(pos[:, :], prefix, gex[:, :], ALU.add))
            link(V.tensor_tensor(pos[:, :], pos[:, :], oh[:, :], ALU.mult))
            link(V.tensor_reduce(mx[:, :], pos[:, :].rearrange("p (e n) -> p n e", n=NB), AX.X, ALU.add))
            link(V.tensor_copy(slot[:, :], mx[:, :]))
            V.tensor_single_scalar(slot_q[:, :], slot[:, :], 7, ALU.arith_shift_right)
            link(V.tensor_single_scalar(slot_r[:, :], slot[:, :], P - 1, ALU.bitwise_and))
            V.tensor_copy(q16[:, :], slot_q[:, :])
            link(V.tensor_copy(r16[:, :], slot_r[:, :]))
            dve.wait_ge(w1_first_split, W1U)
            dve.sem_inc(w1_split, W1P)
            V.tensor_tensor(q_val3, iota16[:, 0:TS].unsqueeze(1).to_broadcast([P, NB, TS]),
                            q16[:, :].unsqueeze(2).to_broadcast([P, NB, TS]), ALU.is_equal).then_inc(q_oh_ready, 1)
            for g in range(4):
                V.tensor_tensor(slot_oh[:, 4 * g:4 * g + 4, :], iota16[:, :].unsqueeze(1).to_broadcast([P, 4, P]),
                                r16[:, 4 * g:4 * g + 4].unsqueeze(2).to_broadcast([P, 4, P]), ALU.is_equal)\
                    .then_inc(slots_ready, 1)

            dve.wait_ge(idx_summed, 1)
            link(V.tensor_copy(idx_f[:, 0:TS], early_ps[:, 0:TS]))
            V.tensor_scalar(g_idx[:, :], idx_f[:, 0:TS], -1.0, 0.0, ALU.add, ALU.max)
            link(V.tensor_scalar(idx_f[:, TS:2 * TS], idx_f[:, 0:TS], 0.0, float(BIG), ALU.is_equal, ALU.mult))
            V.scalar_tensor_tensor(s_idx[:, :], idx_f[:, 0:TS], -1.0, idx_f[:, TS:2 * TS],
                                   ALU.add, ALU.add).then_inc(idx_ready, 1)

            def over_items(ap):
                return ap.unsqueeze(1).to_broadcast([P, TAB, NE])

            le_s, le_e, eq_s, tmp = (ct[:, a * TAB * NE:(a + 1) * TAB * NE].rearrange("p (i e) -> p i e", e=NE)
                                     for a in range(4))
            i_bc = iota[:, 0:TAB].unsqueeze(2).to_broadcast([P, TAB, NE])
            rem, steps, prep, expert, word = (cv[:, a * TAB:(a + 1) * TAB] for a in range(5))
            V.tensor_tensor(le_s, over_items(tst), i_bc, ALU.is_le)
            V.tensor_tensor(le_e, over_items(tend), i_bc, ALU.is_le)
            V.tensor_tensor(eq_s, over_items(tst), i_bc, ALU.is_equal)
            link(V.scalar_tensor_tensor(zed, tst, float(ITEM), cnt, ALU.mult, ALU.add))
            V.tensor_reduce(prep, eq_s[:, :, 0:NE - 1], AX.X, ALU.add)
            V.tensor_reduce(expert, le_e, AX.X, ALU.add)
            link(V.tensor_tensor(tmp, le_s, le_e, ALU.subtract))
            link(V.tensor_tensor(tmp, tmp, over_items(zed), ALU.mult))
            link(V.tensor_reduce(rem, tmp, AX.X, ALU.add))
            link(V.tensor_tensor(rem, rem, before[:, :], ALU.add))
            MORE = len(SIZES) - 1
            tmp_s = ct[:, 0:TAB * MORE].rearrange("p (i m) -> p i m", m=MORE)
            link(V.tensor_tensor(tmp_s, rem.unsqueeze(2).to_broadcast([P, TAB, MORE]),
                                 sizes[:, :].unsqueeze(1).to_broadcast([P, TAB, MORE]), ALU.is_gt))
            V.tensor_reduce(steps, tmp_s, AX.X, ALU.add)
            link(V.tensor_scalar(expert, expert, float(NE - 1), 16.0, ALU.min, ALU.mult))
            link(V.scalar_tensor_tensor(word, prep, 8.0, expert, ALU.mult, ALU.add))
            V.tensor_scalar(ctrl[:, 0:1], tend[:, NE - 1:NE], -1.0, None, ALU.add)
            V.tensor_tensor(ctrl[:, 1:1 + TAB], word, steps, ALU.add).then_inc(ctrl_ready, 1)

            def split_x(i):
                for k in range(KH):
                    part_k = slice(k * ITEM, (k + 1) * ITEM)
                    dve.wait_ge(xr_hi_done, i * KH + (k + 1))
                    V.tensor_tensor(xr_lo[:, part_k], xk_ps[k][:, :], xr_hi[:, part_k].bitcast(F32), ALU.subtract)\
                        .then_inc(xr_lo_done, 1)

            dve.wait_ge(ctrl_ready, 1)
            last_item = load_last(dve)
            next_word = first_word(dve)
            dve.wait_ge(x_rot_done, NB // 2)
            dve.sem_inc(pair_free, RING)
            dve.wait_ge(b1_t_done, 1)
            split_x(0)

            def gated(i, e, c, n):
                dve.wait_ge(a_done, i * NC + (c + 1))
                dve.wait_ge(sig_done, i * NC + (RING + c + 1))
                V.scalar_tensor_tensor(u32[:, c % U_RING, 0:n], pair[c % RING][0][:, 0:n],
                                       b1_t[:, bass.ds(e * (2 * NC) + c, 1)],
                                       sig[:, c % RING, 0:n], ALU.add, ALU.mult).then_inc(pair_free, 1)

            def lo_u(i, c, n):
                dve.wait_ge(u_hi_done, i * NC + (c + 1))
                at = (c % U_RING) * ITEM
                V.tensor_tensor(u_lo[:, at:at + n], u32[:, c % U_RING, 0:n], u_hi[:, at:at + n].bitcast(F32),
                                ALU.subtract).then_inc(u_lo_done, 1)

            def lo_part(parity, at, n_hi):
                dve.wait_ge(w1_hi_done, n_hi)
                V.tensor_tensor(w_lo[:, bass.ds(w_col(parity, 0) + at, PIECE)], w_raw[:, at:at + PIECE],
                                w_hi[:, bass.ds(w_col(parity, 0) + at, PIECE)].bitcast(F32), ALU.subtract)\
                    .then_inc(w1_split, 1)

            def add_rows(i, blocks):
                dve.wait_ge(mm2_done, i + 1)
                dve.wait_ge(xb_done, i + 2)
                for h in range((blocks + 1) // 2):
                    n = min(blocks - 2 * h, 2) * DIM
                    V.tensor_tensor(y_out[:, h * 2 * DIM:h * 2 * DIM + n], y_ps[h][:, 0:n],
                                    xb[:, bass.ds((i & 1) * (NSUB * DIM) + h * 2 * DIM, n)],
                                    ALU.add).then_inc(y_done, 1 if blocks > 2 else 2)

            def item(i, word, blocks, prep):
                n = blocks * P
                e = f_expert(word)
                for c in range(NC):
                    gated(i, e, c, n)
                    if prep:
                        for part in PREP[c]:
                            if part < W1P:
                                lo_part((e + 1) & 1, part * PIECE, e * W1P + (W1P + part + 1))
                    lo_u(i, c, n)
                split_x(i + 1)
                if prep:
                    for part in PREP_LAST:
                        if part < W1P:
                            lo_part((e + 1) & 1, part * PIECE, e * W1P + (W1P + part + 1))
                load_next_word(dve, next_word, i)
                add_rows(i, blocks)

            with dve.Fori(0, MAX_ITEMS) as i:
                with dve.If(i <= last_item):
                    word = this_word(dve, next_word)
                    with dve.If(f_prep(word) > 0):
                        if_blocks(dve, word, lambda blocks: item(i, word, blocks, True))
                    with dve.Else():
                        if_blocks(dve, word, lambda blocks: item(i, word, blocks, False))

        @block.tensor
        def _(pe):
            T = nc.tensor
            pe.wait_ge(consts_ready, 1)
            pe.wait_ge(q_repeated, KH)
            for k in range(KH):
                last = T.matmul(late_ps[:, k * 16:(k + 1) * 16], q_rep[:, k * P:(k + 1) * P], ident[0:13, 0:16],
                                start=True, stop=True)
            last.then_inc(q_spread, 1)

            for f in range(NB // 2):
                if f >= 4:
                    pe.wait_ge(x_t_done, f - 3)
                pe.wait_ge(x_loaded[f // 2], 16)
                for a in range(4):
                    xk = x_tok[:, 4 * (f // 2) + a, :].rearrange("p (m k) -> p k m", k=KH)
                    last = T.transpose(turn_ps[f % 4][:, a * P:(a + 1) * P], xk[:, f % 2], ident[:, :])
                last.then_inc(x_turned, 1)
            pe.wait_ge(small_loaded, 48)
            T.transpose(early_ps[:, 0:P], b1_rows[:, :], ident[:, :]).then_inc(b1_turned, 1)
            pe.wait_ge(rot_t_ready, KH)
            for k in range(KH):
                last = T.matmul(late_ps[:, 256 + k * NE:256 + (k + 1) * NE], rot_t[:, k * P:(k + 1) * P],
                                wr[:, k * NE:(k + 1) * NE], start=True, stop=True)
            last.then_inc(wr_turned, 1)
            pe.wait_ge(wr_ready, 1)
            for g in range(4):
                pe.wait_ge(x_t_done, KH * (g + 1))
                if g >= 2:
                    pe.wait_ge(logits_t_done, g - 1)
                for k in range(KH):
                    last = T.matmul(xk_ps[g % 2][0:NE, :], wr_rot[:, k * NE:(k + 1) * NE],
                                    x_t[:, k, g * 512:(g + 1) * 512], start=(k == 0), stop=(k == KH - 1))
                last.then_inc(logits_t_ready, 1)
            for n in range(NB):
                if n % 4 == 0:
                    pe.wait_ge(logits_t_done, n // 4 + 1)
                last = T.transpose(late_ps[:, n * NE:(n + 1) * NE], logits_t[:, n * P:(n + 1) * P], ident[0:NE, 0:NE])
            last.then_inc(logits_ready, 1)

            def rotate_blocks(b):
                if b >= 4:
                    pe.wait_ge(x_rot_done, b - 3)
                for n in (2 * b, 2 * b + 1):
                    for k in range(KH):
                        at = (n % 2) * DIM + k * P
                        last = T.matmul(turn_ps[b % 4][:, at:at + P], x_t[:, k, n * P:(n + 1) * P],
                                        rot[:, k * P:(k + 1) * P], start=True, stop=True)
                last.then_inc(rot_x_ready, 1)

            pe.wait_ge(rot_ready, KH)
            for b in range(2):
                rotate_blocks(b)
            pe.wait_ge(consts_ready, 8)
            pe.wait_ge(oh_ready, 1)
            T.matmul(xk_ps[1][:, 0:P], lower[:, :], oh[:, :], start=True, stop=True)
            T.matmul(xk_ps[1][:, P:2 * P], ones16[:, :], oh[:, :], start=True, stop=True).then_inc(ranks_ready, 1)
            for b in range(2, NB // 2):
                rotate_blocks(b)
            pe.wait_ge(q_val_ready, 1)
            pe.wait_ge(b1_t_done, 1)
            for n in range(NB):
                if n % 4 == 0:
                    pe.wait_ge(slots_ready, n // 4 + 1)
                last = T.matmul(early_ps[:, 0:TS], slot_oh[:, n, :], q_val[:, n * TS:(n + 1) * TS],
                                start=(n == 0), stop=(n == NB - 1))
            last.then_inc(idx_summed, 1)

            def turn_item(i):
                for s in range(NSUB):
                    pe.wait_ge(gathered[s], i * 16 + 16)
                    for k in range(KH):
                        at = (s * 2 + 1) * DIM + k * P
                        last = T.transpose(xk_ps[k][:, s * P:(s + 1) * P], xg[:, at:at + P], ident[:, :])
                        if s == NSUB - 1:
                            last.then_inc(xg_turned, 1)

            pe.wait_ge(ctrl_ready, 1)
            last_item = load_last(pe)
            next_word = first_word(pe)
            pe.wait_ge(idx_ready, 1)
            turn_item(0)

            def first_product(i, e, parity, n, c):
                if c % 2 == 0:
                    pe.wait_ge(w1_split, e * W1P + (c + 2))
                for ag in (1, 0):
                    pe.wait_ge((pair_free, sig_done)[ag], i * NC + (c + 1))
                    dst = pair[c % RING][ag][:, 0:n]
                    for k in range(KH):
                        if c == 0 and ag == 1:
                            pe.wait_ge(xr_lo_done, i * KH + (k + 1))
                        at = w_col(parity, c // 2) + k * 512 + ag * 256 + (c % 2) * P
                        xh = xr_hi[:, k * ITEM:k * ITEM + n]
                        xl = xr_lo[:, k * ITEM:k * ITEM + n]
                        T.matmul(dst, w_hi[:, at:at + P], xh, start=(k == 0), stop=False)
                        T.matmul(dst, w_hi[:, at:at + P], xl, start=False, stop=False)
                        last = T.matmul(dst, w_lo[:, at:at + P], xh, start=False, stop=(k == KH - 1))
                    last.then_inc((a_done, g_done)[ag], 1)

            def second_product(i, e, parity, blocks, c):
                if c % CPU2 == 0:
                    pe.wait_ge(w2_split, e * W2U + (c // CPU2 + 1))
                if c < NC - LAG:
                    pe.wait_ge(u_lo_done, i * NC + (c + 1))
                at = w_col(parity, W1U + c // CPU2) + (c % CPU2) * DIM
                wv = slice(at, at + DIM)
                if c == 0:
                    for h in range(blocks // 2):
                        T.matmul(y_ps[h][:, :], ones16[0:1, :], zeros16[:, :], start=True, stop=False)
                for s in range(blocks):
                    uv = slice((c % U_RING) * ITEM + s * P, (c % U_RING) * ITEM + (s + 1) * P)
                    dst = y_ps[s // 2][:, (s % 2) * DIM:(s % 2 + 1) * DIM]
                    T.matmul(dst, u_hi[:, uv], w_hi[:, wv], start=(c == 0 and s // 2 == blocks // 2), stop=False)
                    T.matmul(dst, u_hi[:, uv], w_lo[:, wv], start=False, stop=False)
                    last = T.matmul(dst, u_lo[:, uv], w_hi[:, wv], start=False,
                                    stop=(c == NC - 1 and (s % 2 == 1 or s == blocks - 1)))
                if c == NC - 1:
                    last.then_inc(mm2_done, 1)

            def item(i, word, parity, size):
                e = f_expert(word)
                blocks = BLOCKS[size]
                for c in range(NC):
                    first_product(i, e, parity, SIZES[size], c)
                    if c == NC - 1:
                        turn_item(i + 1)
                    if LAG <= c < NC - 2:
                        second_product(i, e, parity, blocks, c - LAG)
                for c in range(NC - 2 - LAG, NC - LAG):
                    second_product(i, e, parity, blocks, c)
                load_next_word(pe, next_word, i)
                pe.wait_ge(u_lo_done, i * NC + NC)
                for c in range(NC - LAG, NC):
                    second_product(i, e, parity, blocks, c)

            def item_of_any_size(i, word, parity, low, high):
                if low == high:
                    item(i, word, parity, low)
                    return
                middle = (low + high + 1) // 2
                with pe.If(f_size(word) < middle):
                    item_of_any_size(i, word, parity, low, middle - 1)
                with pe.Else():
                    item_of_any_size(i, word, parity, middle, high)

            with pe.Fori(0, MAX_ITEMS) as i:
                with pe.If(i <= last_item):
                    word = this_word(pe, next_word)
                    with pe.If((f_expert(word) & 1) < 1):
                        item_of_any_size(i, word, 0, 0, len(SIZES) - 1)
                    with pe.Else():
                        item_of_any_size(i, word, 1, 0, len(SIZES) - 1)


_INS = ['x', 'cond_256', 'L0_cond_q_right', 'L0_cond_spectral_gate', 'L0_ffn_router_w', 'L0_ffn_router_b',
        'L0_ffn_w1', 'L0_ffn_b1', 'L0_ffn_w2', 'L0_ffn_b2']
_OUTS = [((8, 256, 256), 'float32')]


def kernel(**inputs):
    import numpy as _np
    import concourse.bacc as _bacc
    from concourse import mybir as _mybir
    from concourse.bass_utils import run_bass_kernel_spmd as _run

    nc = _bacc.Bacc("TRN2", target_bir_lowering=False, num_devices=1)
    arrays, args = {}, []
    for name in _INS:
        a = _np.ascontiguousarray(inputs[name])
        arrays[f"in_{name}_dram"] = a
        args.append(nc.dram_tensor(f"in_{name}_dram", a.shape, _mybir.dt.from_np(a.dtype), kind="ExternalInput").ap())
    for i, (shape, dtype) in enumerate(_OUTS):
        dt = _mybir.dt.from_np(_np.dtype(dtype))
        args.append(nc.dram_tensor(f"out_{i}_dram", shape, dt, kind="ExternalOutput").ap())
    adaln_moe_ffn_kernel(nc, *args)
    r = _run(nc, [arrays], core_ids=[0])
    got = tuple(r.results[0][f"out_{i}_dram"] for i in range(len(_OUTS)))
    return got[0]
```
